# Optimizing a Trainium2 kernel written in Bass

```python
import numpy as np
import jax
import jax.numpy as jnp

def _softmax(x, axis=-1):
    return jax.nn.softmax(x, axis=axis)

def _gelu(x):
    return jax.nn.gelu(x, approximate=True)

def _silu(x):
    return jax.nn.silu(x)

def _sigmoid(x):
    return jax.nn.sigmoid(x)

def _layernorm(x, axis=-1, eps=1e-05):
    m = jnp.mean(x, axis=axis, keepdims=True)
    v = jnp.var(x, axis=axis, keepdims=True)
    return (x - m) / jnp.sqrt(v + eps)

def _scatter_add(tgt, idx, src, axis=0):
    return tgt.at[idx].add(src)

def _segment_sum(src, seg, n):
    return jax.ops.segment_sum(src, seg, n)
kernel_name = 'mk_vit_tower_d1_tok_img768_r4_897a0b'

def setup_inputs(seed: int=0):
    np.random.seed(seed)
    _w = jnp.asarray

    def _rec_inputs():
        import jax
        import jax.numpy as jnp
        _rk = jax.random.key(seed)
        x = -0.000356955 + 1 * jax.random.normal(jax.random.fold_in(_rk, 1), (64, 3, 128, 128), jnp.float32)
        return x
    x = _rec_inputs()

    def _L0_tok_setup():
        import jax, jax.numpy as jnp
        import numpy as np
        NBITS = 8
        QN = -2 ** (NBITS - 1)
        QP = 2 ** (NBITS - 1) - 1
        PATCH = 16

        def _ste_round(v):
            return v + jax.lax.stop_gradient(jnp.round(v) - v)

        def lsq_quant(x, alpha, qn, qp):
            return _ste_round(jnp.clip(x / alpha, qn, qp)) * alpha
        key = jax.random.key(seed)
        k1, k2 = jax.random.split(key)
        x = jax.random.normal(k1, (128, 3, 224, 224), jnp.float32)
        W = jax.random.normal(k2, (192, 3, 16, 16), jnp.float32) * 0.02
        b = jnp.zeros((192,), jnp.float32)
        alpha_w = (2.0 * jnp.mean(jnp.abs(W)) / jnp.sqrt(jnp.float32(QP))).astype(jnp.float32)
        alpha_a = (2.0 * jnp.mean(jnp.abs(x)) / jnp.sqrt(jnp.float32(QP))).astype(jnp.float32)
        return {'x': x, 'W': W, 'b': b, 'alpha_w': alpha_w, 'alpha_a': alpha_a}
    _L0_tok_all = _L0_tok_setup()
    _L0_tok_in = {k: v for k, v in _L0_tok_all.items() if k in ('W', 'b', 'alpha_w', 'alpha_a')}
    del _L0_tok_all

    def _L0_attn_setup():
        import jax, jax.numpy as jnp
        import numpy as np
        D_MODEL = 192
        STATE_N = 16
        BATCH = 8
        SEQ = 512

        def _forward(x, A_log, D_param, B_proj_w, C_proj_w, delta_w, delta_b, in_w, in_b, out_w, out_b, conv_w, conv_b):
            A = -jnp.exp(A_log)
            xz = jnp.einsum('bld,ed->ble', x, in_w) + in_b
            x_in, z = jnp.split(xz, 2, axis=-1)
            x_c = jax.lax.conv_general_dilated(jnp.transpose(x_in, (0, 2, 1)), conv_w, window_strides=(1,), padding=((1, 1),), feature_group_count=x.shape[-1], dimension_numbers=('NCH', 'OIH', 'NCH'))
            x_conv = jnp.transpose(x_c, (0, 2, 1)) + conv_b
            x_conv = jax.nn.silu(x_conv)
            delta = jax.nn.softplus(jnp.einsum('bld,ed->ble', x_conv, delta_w) + delta_b)
            B_sel = jnp.einsum('bld,nd->bln', x_conv, B_proj_w)
            C_sel = jnp.einsum('bld,nd->bln', x_conv, C_proj_w)
            Bsz, L, D = x.shape
            N = A.shape[1]

            def step(h, t_in):
                dt, b_t, c_t, x_t = t_in
                A_bar = jnp.exp(dt[:, :, None] * A[None, :, :])
                h = A_bar * h + dt[:, :, None] * b_t[:, None, :] * x_t[:, :, None]
                y_t = jnp.sum(h * c_t[:, None, :], axis=-1)
                return (h, y_t)
            xs = (jnp.transpose(delta, (1, 0, 2)), jnp.transpose(B_sel, (1, 0, 2)), jnp.transpose(C_sel, (1, 0, 2)), jnp.transpose(x_conv, (1, 0, 2)))
            h0 = jnp.zeros((Bsz, D, N), dtype=x.dtype)
            _, ys = jax.lax.scan(step, h0, xs)
            y = jnp.transpose(ys, (1, 0, 2))
            y = y + x_conv * D_param[None, None, :]
            y = y * jax.nn.silu(z)
            return jnp.einsum('bld,ed->ble', y, out_w) + out_b
        key = jax.random.key(seed)
        ks = jax.random.split(key, 12)
        d, n = (D_MODEL, STATE_N)
        s = 0.02
        inp = {'x': jax.random.normal(ks[0], (BATCH, SEQ, d), dtype=jnp.float32), 'A_log': jnp.log(jnp.tile(jnp.arange(1, n + 1, dtype=jnp.float32)[None, :], (d, 1))), 'D_param': jnp.ones((d,), dtype=jnp.float32), 'B_proj_w': jax.random.normal(ks[1], (n, d), dtype=jnp.float32) * s, 'C_proj_w': jax.random.normal(ks[2], (n, d), dtype=jnp.float32) * s, 'delta_w': jax.random.normal(ks[3], (d, d), dtype=jnp.float32) * s, 'delta_b': jax.random.normal(ks[4], (d,), dtype=jnp.float32) * s, 'in_w': jax.random.normal(ks[5], (2 * d, d), dtype=jnp.float32) * s, 'in_b': jax.random.normal(ks[6], (2 * d,), dtype=jnp.float32) * s, 'out_w': jax.random.normal(ks[7], (d, d), dtype=jnp.float32) * s, 'out_b': jax.random.normal(ks[8], (d,), dtype=jnp.float32) * s, 'conv_w': jax.random.normal(ks[9], (d, 1, 3), dtype=jnp.float32) * s, 'conv_b': jax.random.normal(ks[10], (d,), dtype=jnp.float32) * s}
        return inp
    _L0_attn_all = _L0_attn_setup()
    _L0_attn_in = {k: v for k, v in _L0_attn_all.items() if k in ('A_log', 'D_param', 'B_proj_w', 'C_proj_w', 'delta_w', 'delta_b', 'in_w', 'in_b', 'out_w', 'out_b', 'conv_w', 'conv_b')}
    del _L0_attn_all

    def _L0_ffn_setup():
        import jax, jax.numpy as jnp
        import numpy as np
        from jax import lax
        DIM = 192
        INTER = 128
        E = 8
        G = 4
        TOPK_G = 2
        TOPK = 2
        ROUTE_SCALE = 1.0

        def _gate(x2, gate_weight, gate_bias):
            T = x2.shape[0]
            scores = jax.nn.sigmoid(x2 @ gate_weight.T)
            s = scores + gate_bias
            sv = s.reshape(T, G, E // G)
            top2, _ = lax.top_k(sv, 2)
            group_scores = top2.sum(-1)
            _, gidx = lax.top_k(group_scores, TOPK_G)
            gmask = jnp.zeros((T, G), bool).at[jnp.arange(T)[:, None], gidx].set(True)
            masked = jnp.where(gmask[:, :, None], sv, -jnp.inf).reshape(T, E)
            _, idx = lax.top_k(masked, TOPK)
            w = jnp.take_along_axis(scores, idx, axis=1)
            w = w / (w.sum(-1, keepdims=True) + 1e-06) * ROUTE_SCALE
            return (w, idx)
        key = jax.random.key(seed)
        ks = jax.random.split(key, 9)
        s = 1.0 / np.sqrt(DIM)
        si = 1.0 / np.sqrt(INTER)
        return {'x': jax.random.normal(ks[0], (4, 1024, DIM), jnp.float32), 'gate_weight': jax.random.uniform(ks[1], (E, DIM), jnp.float32, -s, s), 'gate_bias': jnp.zeros((E,), jnp.float32), 'w1': jax.random.uniform(ks[2], (E, INTER, DIM), jnp.float32, -s, s), 'w2': jax.random.uniform(ks[3], (E, DIM, INTER), jnp.float32, -si, si), 'w3': jax.random.uniform(ks[4], (E, INTER, DIM), jnp.float32, -s, s), 'sw1': jax.random.uniform(ks[5], (INTER, DIM), jnp.float32, -s, s), 'sw2': jax.random.uniform(ks[6], (DIM, INTER), jnp.float32, -si, si), 'sw3': jax.random.uniform(ks[7], (INTER, DIM), jnp.float32, -s, s)}
    _L0_ffn_all = _L0_ffn_setup()
    _L0_ffn_in = {k: v for k, v in _L0_ffn_all.items() if k in ('gate_weight', 'gate_bias', 'w1', 'w2', 'w3', 'sw1', 'sw2', 'sw3')}
    del _L0_ffn_all
    return {'x': x, 'L0_tok_W': _L0_tok_in['W'], 'L0_tok_b': _L0_tok_in['b'], 'L0_tok_alpha_w': _L0_tok_in['alpha_w'], 'L0_tok_alpha_a': _L0_tok_in['alpha_a'], 'L0_attn_A_log': _L0_attn_in['A_log'], 'L0_attn_D_param': _L0_attn_in['D_param'], 'L0_attn_B_proj_w': _L0_attn_in['B_proj_w'], 'L0_attn_C_proj_w': _L0_attn_in['C_proj_w'], 'L0_attn_delta_w': _L0_attn_in['delta_w'], 'L0_attn_delta_b': _L0_attn_in['delta_b'], 'L0_attn_in_w': _L0_attn_in['in_w'], 'L0_attn_in_b': _L0_attn_in['in_b'], 'L0_attn_out_w': _L0_attn_in['out_w'], 'L0_attn_out_b': _L0_attn_in['out_b'], 'L0_attn_conv_w': _L0_attn_in['conv_w'], 'L0_attn_conv_b': _L0_attn_in['conv_b'], 'L0_ffn_gate_weight': _L0_ffn_in['gate_weight'], 'L0_ffn_gate_bias': _L0_ffn_in['gate_bias'], 'L0_ffn_w1': _L0_ffn_in['w1'], 'L0_ffn_w2': _L0_ffn_in['w2'], 'L0_ffn_w3': _L0_ffn_in['w3'], 'L0_ffn_sw1': _L0_ffn_in['sw1'], 'L0_ffn_sw2': _L0_ffn_in['sw2'], 'L0_ffn_sw3': _L0_ffn_in['sw3']}

def reference(x, L0_tok_W, L0_tok_b, L0_tok_alpha_w, L0_tok_alpha_a, L0_attn_A_log, L0_attn_D_param, L0_attn_B_proj_w, L0_attn_C_proj_w, L0_attn_delta_w, L0_attn_delta_b, L0_attn_in_w, L0_attn_in_b, L0_attn_out_w, L0_attn_out_b, L0_attn_conv_w, L0_attn_conv_b, L0_ffn_gate_weight, L0_ffn_gate_bias, L0_ffn_w1, L0_ffn_w2, L0_ffn_w3, L0_ffn_sw1, L0_ffn_sw2, L0_ffn_sw3):
    import jax
    import jax.numpy as jnp

    def _L0_tok_ref(x, W, b, alpha_w, alpha_a):
        import jax, jax.numpy as jnp
        import numpy as np
        NBITS = 8
        QN = -2 ** (NBITS - 1)
        QP = 2 ** (NBITS - 1) - 1
        PATCH = 16

        def _ste_round(v):
            return v + jax.lax.stop_gradient(jnp.round(v) - v)

        def lsq_quant(x, alpha, qn, qp):
            return _ste_round(jnp.clip(x / alpha, qn, qp)) * alpha
        xq = lsq_quant(x, alpha_a, QN, QP)
        wq = lsq_quant(W, alpha_w, QN, QP)
        y = jax.lax.conv_general_dilated(xq, wq, window_strides=(PATCH, PATCH), padding='VALID', dimension_numbers=('NCHW', 'OIHW', 'NCHW'))
        y = y + b[None, :, None, None]
        B, E, Hp, Wp = y.shape
        return jnp.transpose(y.reshape(B, E, Hp * Wp), (0, 2, 1))

    def _L0_attn_ref(x, A_log, D_param, B_proj_w, C_proj_w, delta_w, delta_b, in_w, in_b, out_w, out_b, conv_w, conv_b):
        import jax, jax.numpy as jnp
        import numpy as np
        D_MODEL = 192
        STATE_N = 16
        BATCH = 8
        SEQ = 512

        def _forward(x, A_log, D_param, B_proj_w, C_proj_w, delta_w, delta_b, in_w, in_b, out_w, out_b, conv_w, conv_b):
            A = -jnp.exp(A_log)
            xz = jnp.einsum('bld,ed->ble', x, in_w) + in_b
            x_in, z = jnp.split(xz, 2, axis=-1)
            x_c = jax.lax.conv_general_dilated(jnp.transpose(x_in, (0, 2, 1)), conv_w, window_strides=(1,), padding=((1, 1),), feature_group_count=x.shape[-1], dimension_numbers=('NCH', 'OIH', 'NCH'))
            x_conv = jnp.transpose(x_c, (0, 2, 1)) + conv_b
            x_conv = jax.nn.silu(x_conv)
            delta = jax.nn.softplus(jnp.einsum('bld,ed->ble', x_conv, delta_w) + delta_b)
            B_sel = jnp.einsum('bld,nd->bln', x_conv, B_proj_w)
            C_sel = jnp.einsum('bld,nd->bln', x_conv, C_proj_w)
            Bsz, L, D = x.shape
            N = A.shape[1]

            def step(h, t_in):
                dt, b_t, c_t, x_t = t_in
                A_bar = jnp.exp(dt[:, :, None] * A[None, :, :])
                h = A_bar * h + dt[:, :, None] * b_t[:, None, :] * x_t[:, :, None]
                y_t = jnp.sum(h * c_t[:, None, :], axis=-1)
                return (h, y_t)
            xs = (jnp.transpose(delta, (1, 0, 2)), jnp.transpose(B_sel, (1, 0, 2)), jnp.transpose(C_sel, (1, 0, 2)), jnp.transpose(x_conv, (1, 0, 2)))
            h0 = jnp.zeros((Bsz, D, N), dtype=x.dtype)
            _, ys = jax.lax.scan(step, h0, xs)
            y = jnp.transpose(ys, (1, 0, 2))
            y = y + x_conv * D_param[None, None, :]
            y = y * jax.nn.silu(z)
            return jnp.einsum('bld,ed->ble', y, out_w) + out_b
        return _forward(x, A_log, D_param, B_proj_w, C_proj_w, delta_w, delta_b, in_w, in_b, out_w, out_b, conv_w, conv_b)

    def _L0_ffn_ref(x, gate_weight, gate_bias, w1, w2, w3, sw1, sw2, sw3):
        import jax, jax.numpy as jnp
        import numpy as np
        from jax import lax
        DIM = 192
        INTER = 128
        E = 8
        G = 4
        TOPK_G = 2
        TOPK = 2
        ROUTE_SCALE = 1.0

        def _gate(x2, gate_weight, gate_bias):
            T = x2.shape[0]
            scores = jax.nn.sigmoid(x2 @ gate_weight.T)
            s = scores + gate_bias
            sv = s.reshape(T, G, E // G)
            top2, _ = lax.top_k(sv, 2)
            group_scores = top2.sum(-1)
            _, gidx = lax.top_k(group_scores, TOPK_G)
            gmask = jnp.zeros((T, G), bool).at[jnp.arange(T)[:, None], gidx].set(True)
            masked = jnp.where(gmask[:, :, None], sv, -jnp.inf).reshape(T, E)
            _, idx = lax.top_k(masked, TOPK)
            w = jnp.take_along_axis(scores, idx, axis=1)
            w = w / (w.sum(-1, keepdims=True) + 1e-06) * ROUTE_SCALE
            return (w, idx)
        B, S, D = x.shape
        x2 = x.reshape(-1, D)
        T = x2.shape[0]
        weights, indices = _gate(x2, gate_weight, gate_bias)
        cw = jnp.zeros((T, E), x.dtype).at[jnp.arange(T)[:, None], indices].add(weights)
        h1 = jnp.einsum('td,eid->tei', x2, w1)
        h3 = jnp.einsum('td,eid->tei', x2, w3)
        h = jax.nn.silu(h1) * h3
        y = jnp.einsum('tei,edi,te->td', h, w2, cw)
        z = jax.nn.silu(x2 @ sw1.T) * (x2 @ sw3.T) @ sw2.T
        return (y + z).reshape(B, S, D)
    h = _L0_tok_ref(x, L0_tok_W, L0_tok_b, L0_tok_alpha_w, L0_tok_alpha_a)
    h = h + _L0_attn_ref(_layernorm(h, axis=-1), L0_attn_A_log, L0_attn_D_param, L0_attn_B_proj_w, L0_attn_C_proj_w, L0_attn_delta_w, L0_attn_delta_b, L0_attn_in_w, L0_attn_in_b, L0_attn_out_w, L0_attn_out_b, L0_attn_conv_w, L0_attn_conv_b)
    h = h + _L0_ffn_ref(_layernorm(h, axis=-1), L0_ffn_gate_weight, L0_ffn_gate_bias, L0_ffn_w1, L0_ffn_w2, L0_ffn_w3, L0_ffn_sw1, L0_ffn_sw2, L0_ffn_sw3)
    return h

_drawn_inputs = setup_inputs


def setup_inputs(seed=0):
    import zlib

    import numpy as np

    out = dict(_drawn_inputs(seed))
    spreads = {'L0_tok_b': (0.0, 0.1), 'L0_attn_D_param': (1.0, 0.6), 'L0_ffn_gate_bias': (0.0, 0.357)}
    factors = {'L0_attn_A_log': 8.0,
     'L0_attn_B_proj_w': 8.0,
     'L0_attn_C_proj_w': 8.0,
     'L0_attn_delta_w': 8.0,
     'L0_attn_delta_b': 8.0,
     'L0_attn_in_w': 8.0,
     'L0_attn_in_b': 8.0,
     'L0_attn_out_w': 8.0,
     'L0_attn_conv_w': 8.0,
     'L0_attn_conv_b': 8.0,
     'L0_attn_out_b': 6.751}
    for name, (base, spread) in spreads.items():
        noise = np.random.default_rng([zlib.crc32(name.encode()), seed]).standard_normal(out[name].shape)
        drawn = base * np.exp(spread * noise) if base else spread * noise
        out[name] = jnp.asarray(drawn.astype(out[name].dtype))
    for name, factor in factors.items():
        out[name] = (out[name] * factor).astype(out[name].dtype)
    return out
```

```python
from contextlib import ExitStack

import concourse.bass as bass
from concourse import mybir

F32 = mybir.dt.float32
BF16 = mybir.dt.bfloat16
ALU = mybir.AluOpType
ACT = mybir.ActivationFunctionType
AX = mybir.AxisListType

P = 128
D = 192
DR = D - P
L = 64
CH = 512
HALF = CH // 2
PK = CH + HALF
TT = CH // P
KT = 768 // P
N = 16
E = 8
EX = E + 1
ROUND = 1.5 * 2 ** 23
LN_EPS = 1e-5

UNITS = [u for m in range(0, N, 2) for u in (("A", m), ("A", m + 1), ("B", m))]
NU = len(UNITS)
A_RING, H_RING, C_RING, Y_RING = 3, 3, 2, 3

COLS = ["in_b_x", "in_b_z", "conv_w0", "conv_w1", "conv_w2", "conv_b", "delta_b", "D_param"]
NCOL = 2 * len(COLS)


def build(nc, t, out):
    n_chunks = t["x"].shape[0]
    ctx = ExitStack()
    with ctx:
        def sb(name, shape, dt=F32):
            return ctx.enter_context(nc.sbuf_tensor(name, shape, dt))

        ident = sb("ident", [P, P])
        sel = sb("sel", [96, 2 * N, P], BF16)
        cols = sb("cols", [P, NCOL])
        col_half = sb("col_half", [P, NCOL])
        conv_bias = sb("conv_bias", [P, 2])
        alphas = sb("alphas", [P, 2])
        inv_alpha = sb("inv_alpha", [P, 2])
        alpha_prod = sb("alpha_prod", [P, 1])
        round_col = sb("round_col", [P, 1])
        a_log = sb("a_log", [P, 2 * N])
        a_neg = sb("a_neg", [P, 2 * N])
        tok_wq = sb("tok_wq", [P, KT * D], BF16)
        tok_b = sb("tok_b", [P, 2 * D])
        out_b = sb("out_b", [P, TT * D])
        in_w = sb("in_w", [P, 2, 2 * D])
        delta_w = sb("delta_w", [P, 2, D])
        bc_w = sb("bc_w", [P, 2, 96])
        out_w = sb("out_w", [P, 2, D])
        gate_w = sb("gate_w", [P, 2, E])
        gate_b = sb("gate_b", [P, TT * E])
        before4 = sb("before4", [P, 16])
        before8 = sb("before8", [P, 64])
        w1 = sb("w1", [P, 2, EX, P])
        w3 = sb("w3", [P, 2, EX, P])
        w2 = sb("w2", [P, EX, D])
        neg_half = sb("neg_half", [P, TT])

        xs = sb("xs", [P, KT * CH])
        xq = sb("xq", [P, KT * CH], BF16)
        h0 = [sb(f"h0_{i}", [P, TT, D]) for i in range(2)]
        h0b = sb("h0b", [P, TT, D])
        stats = [sb(f"stats{i}", [P, TT, 6]) for i in range(2)]
        mv = [sb(f"mv{i}", [P, TT, 2]) for i in range(2)]
        vare = [sb(f"vare{i}", [P, TT]) for i in range(2)]
        rstd = [sb(f"rstd{i}", [P, TT]) for i in range(2)]
        xn = [sb(f"xn{i}", [P, TT, D]) for i in range(2)]
        xt = [sb(f"xt{i}", [P, CH]) for i in range(2)]
        xtr = [sb(f"xtr{i}", [DR, CH]) for i in range(2)]
        xin = sb("xin", [P, PK])
        cv = sb("cv", [P, PK])
        cvt = sb("cvt", [P, PK])
        zh = sb("zh", [P, PK])
        zt = sb("zt", [P, PK])
        sp_relu = sb("sp_relu", [P, PK])
        sp_ln = sb("sp_ln", [P, PK])
        xc = [sb(f"xc{i}", [P, PK]) for i in range(2)]
        zs = [sb(f"zs{i}", [P, PK]) for i in range(2)]
        dt = [sb(f"dt{i}", [P, PK]) for i in range(2)]
        ut = [sb(f"ut{i}", [P, PK]) for i in range(2)]
        bc = [sb(f"bc{i}", [96, CH], BF16) for i in range(2)]
        split_r = sb("split_r", [96, CH])
        split_m = sb("split_m", [96, CH], BF16)
        decay = [sb(f"decay{i}", [P, CH]) for i in range(A_RING)]
        hs = [sb(f"hs{i}", [P, CH]) for i in range(H_RING)]
        cs = [sb(f"cs{i}", [P, CH]) for i in range(C_RING)]
        hc = [sb(f"hc{i}", [P, CH]) for i in range(Y_RING)]
        ys = sb("ys", [P, PK])
        yg = sb("yg", [P, PK])
        h1 = sb("h1", [P, TT, D])
        gt = sb("gt", [P, TT * E])
        score = sb("score", [P, TT, E])
        biased = sb("biased", [P, TT, E])
        gsum = sb("gsum", [P, TT, 4])
        g_gt = sb("g_gt", [P, TT, 4, 4])
        g_ge = sb("g_ge", [P, TT, 4, 4])
        g_rank = sb("g_rank", [P, TT, 4])
        g_sel = sb("g_sel", [P, TT, 4])
        e_gt = sb("e_gt", [P, TT, 8, 8])
        e_ge = sb("e_ge", [P, TT, 8, 8])
        e_rank = sb("e_rank", [P, TT, E])
        e_sel = sb("e_sel", [P, TT, E])
        e_w = sb("e_w", [P, TT, E])
        wsum = sb("wsum", [P, TT])
        winv = sb("winv", [P, TT])
        cw3 = sb("cw3", [P, TT, 3, 32])
        cws = sb("cws", [96, CH], BF16)
        csplit_m = sb("csplit_m", [96, CH], BF16)
        cwr = sb("cwr", [P, E, CH])
        tok_w = cwr[:].rearrange("p e t -> p (e t)")[:, 0:KT * D]
        et = sb("et", [P, CH])
        eq = sb("eq", [P, CH])
        csplit_r = eq[0:96, :]
        eg = [sb(f"eg{i}", [P, CH]) for i in range(2)]
        eh = [sb(f"eh{i}", [P, CH]) for i in range(2)]

        pb = ctx.enter_context(nc.psum_tensor("pb", [P, CH], F32))
        pc = ctx.enter_context(nc.psum_tensor("pc", [P, CH], F32))
        py = ctx.enter_context(nc.psum_tensor("py", [P, 2, 512], F32))
        pf = ctx.enter_context(nc.psum_tensor("pf", [P, 4, 512], F32))
        F = [pf[:, i, :] for i in range(4)]

        def sem(name):
            return ctx.enter_context(nc.semaphore(name))

        s_w_in = sem("w_in")
        s_consts = sem("consts")
        s_tokw_scaled = sem("tokw_scaled")
        s_tokw_clamped = sem("tokw_clamped")
        s_tokw_ready = sem("tokw_ready")
        s_avec_exp = sem("avec_exp")
        s_avec_ready = sem("avec_ready")
        s_cols_ready = sem("cols_ready")
        s_prep = sem("prep")
        s_x_in = sem("x_in")
        s_x_scaled = sem("x_scaled")
        s_xq_top = sem("xq_top")
        s_xq_ready = sem("xq_ready")
        s_conv_done = sem("conv_done")
        s_h0_ready = sem("h0_ready")
        s_stats_seen = sem("stats_seen")
        s_st1 = sem("st1")
        s_mv1 = sem("mv1")
        s_ve1 = sem("ve1")
        s_rs1 = sem("rs1")
        s_xn1 = sem("xn1")
        s_tr1 = sem("tr1")
        s_xt1a = sem("xt1a")
        s_xt1b = sem("xt1b")
        s_px_done = sem("px_done")
        s_pz_done = sem("pz_done")
        s_xin_ready = sem("xin_ready")
        s_cv0_ready = sem("cv0_ready")
        s_cv1_ready = sem("cv1_ready")
        s_cv2_ready = sem("cv2_ready")
        s_cvt_ready = sem("cvt_ready")
        s_xc_ready = sem("xc_ready")
        s_zh_ready = sem("zh_ready")
        s_zt_ready = sem("zt_ready")
        s_zs_ready = sem("zs_ready")
        s_lower_rows = sem("lower_rows")
        s_pd_done = sem("pd_done")
        s_pbc_done = sem("pbc_done")
        s_relu_ready = sem("relu_ready")
        s_abs_ready = sem("abs_ready")
        s_spe_ready = sem("spe_ready")
        s_spl_ready = sem("spl_ready")
        s_dt_ready = sem("dt_ready")
        s_ut_ready = sem("ut_ready")
        s_bc_hi = sem("bc_hi")
        s_bc_r = sem("bc_r")
        s_bc_m = sem("bc_m")
        s_bc_mid = sem("bc_mid")
        s_bc_ready = sem("bc_ready")
        s_decay_ready = sem("decay_ready")
        s_b_spread = sem("b_spread")
        s_c_spread = sem("c_spread")
        s_b_times_u = sem("b_times_u")
        s_h_ready = sem("h_ready")
        s_c_copied = sem("c_copied")
        s_hc_ready = sem("hc_ready")
        s_y_added = sem("y_added")
        s_ys_ready = sem("ys_ready")
        s_yg_ready = sem("yg_ready")
        s_po_done = sem("po_done")
        s_h0b_ready = sem("h0b_ready")
        s_h1_ready = sem("h1_ready")
        s_st2 = sem("st2")
        s_mv2 = sem("mv2")
        s_ve2 = sem("ve2")
        s_rs2 = sem("rs2")
        s_xn2 = sem("xn2")
        s_tr2 = sem("tr2")
        s_xt2a = sem("xt2a")
        s_xt2b = sem("xt2b")
        s_pg_done = sem("pg_done")
        s_gt_ready = sem("gt_ready")
        s_score_ready = sem("score_ready")
        s_biased_ready = sem("biased_ready")
        s_gsum_ready = sem("gsum_ready")
        s_ggt_ready = sem("ggt_ready")
        s_gge_ready = sem("gge_ready")
        s_gm_ready = sem("gm_ready")
        s_grank_ready = sem("grank_ready")
        s_gsel_ready = sem("gsel_ready")
        s_egt_ready = sem("egt_ready")
        s_ege_ready = sem("ege_ready")
        s_em_ready = sem("em_ready")
        s_ems_ready = sem("ems_ready")
        s_erank_ready = sem("erank_ready")
        s_esel_ready = sem("esel_ready")
        s_esel2_ready = sem("esel2_ready")
        s_ew_ready = sem("ew_ready")
        s_wsum_ready = sem("wsum_ready")
        s_weps_ready = sem("weps_ready")
        s_winv_ready = sem("winv_ready")
        s_cw_ready = sem("cw_ready")
        s_cwt_done = sem("cwt_done")
        s_cw_hi = sem("cw_hi")
        s_cw_r = sem("cw_r")
        s_cw_m = sem("cw_m")
        s_cw_mid = sem("cw_mid")
        s_cw_parts = sem("cw_parts")
        s_cw_spread = sem("cw_spread")
        s_cw_copied = sem("cw_copied")
        s_e1_done = sem("e1_done")
        s_e3_done = sem("e3_done")
        s_et_ready = sem("et_ready")
        s_eq_ready = sem("eq_ready")
        s_eg_ready = sem("eg_ready")
        s_eh_ready = sem("eh_ready")
        s_e2_done = sem("e2_done")
        s_out_ready = sem("out_ready")
        s_out_stored = sem("out_stored")

        def wait(eng, sem, value):
            if isinstance(value, int) and value <= 0:
                return
            eng.wait_ge(sem, value)

        block = ctx.enter_context(nc.Block())
        A, B = slice(0, CH), slice(CH, PK)
        halves = [(slice(0, 64), slice(0, HALF)), (slice(64, 128), slice(HALF, CH))]

        def col(tile, name, part):
            i = 2 * COLS.index(name) + part
            return tile[:, i:i + 1]

        def images(ap):
            return ap.rearrange("p (m l) -> p m l", l=L)

        def bank_pair(i):
            return F[2 + i][:, 0:2 * D].rearrange("p (t d) -> p t d", d=D)

        def tok_tile(tt):
            return F[2 + tt // 2][:, (tt % 2) * D:(tt % 2) * D + D]

        WEIGHTS = [(ident, t["ident"]), (sel, t["sel"]), (cols, t["cols"]), (alphas, t["alphas"]), (a_log, t["a_log"]),
                   (tok_w, t["tok_w"]), (tok_b, t["tok_b"]), (out_b, t["out_b"]), (in_w, t["in_w"]),
                   (delta_w, t["delta_w"]), (bc_w, t["bc_w"]), (out_w, t["out_w"]), (gate_w, t["gate_w"]),
                   (gate_b, t["gate_b"]), (before4, t["before4"]), (before8, t["before8"]), (w1, t["w1"]),
                   (w3, t["w3"]), (w2, t["w2"])]
        W_ALL = 16 * len(WEIGHTS)

        def over_chunks(eng, first, middle, last):
            first()
            with eng.Fori(0, (n_chunks - 2) // 2) as k:
                middle(k * 2 + 1, 1)
                middle(k * 2 + 2, 0)
            last()

        @block.sync
        def _(sp):
            for tile, src in WEIGHTS:
                sp.dma_start(tile if tile is tok_w else tile[:], src).then_inc(s_w_in, 16)

            def load_x(c):
                wait(sp, s_xq_top, c)
                sp.dma_start(xs[:], t["x"][c]).then_inc(s_x_in, 16)

            def store(c):
                sp.wait_ge(s_out_ready, c + 1)
                sp.dma_start(out[c], h1[:]).then_inc(s_out_stored, 16)

            sp.sem_inc(s_out_stored, 1)
            load_x(0)
            load_x(1)
            load_x(2)
            with sp.Fori(0, n_chunks - 3) as k:
                store(k)
                load_x(k + 3)
            for c in range(n_chunks - 3, n_chunks):
                store(c)
            sp.wait_ge(s_out_stored, 16 * n_chunks + 1)

        @block.tensor
        def _(pe):
            mm = nc.tensor.matmul

            def project(dst_a, dst_b, w, m0, rhs_a, rhs_b):
                mm(dst_a, w[:, 0, m0:m0 + P], rhs_a, start=True, stop=False)
                mm(dst_a, w[0:DR, 1, m0:m0 + P], rhs_b, start=False, stop=True)
                for rows, toks in halves:
                    mm(dst_b[rows, :], w[:, 0, m0 + P:m0 + D], rhs_a[:, toks], start=True, stop=False)
                    last = mm(dst_b[rows, :], w[0:DR, 1, m0 + P:m0 + D], rhs_b[:, toks], start=False, stop=True)
                return last

            def remainder(dst, w, rhs, half):
                rows, toks = halves[half]
                return mm(dst[:, toks], w[rows, :], rhs[rows, B], start=False, stop=True,
                          skip_group_check=True)

            def turn(c, i, before):
                pe.wait_ge([s_xn1, s_xn2][i], c + 1)
                for sem, value in before:
                    wait(pe, sem, value)
                for tt in range(TT):
                    nc.tensor.transpose(F[0][:, tt * P:(tt + 1) * P], xn[i][:, tt, 0:P], ident[:])
                for tt in range(TT):
                    last = nc.tensor.transpose(F[1][0:DR, tt * P:(tt + 1) * P], xn[i][:, tt, P:D], ident[:])
                last.then_inc([s_tr1, s_tr2][i], 1)

            def embed(c):
                pe.wait_ge(s_xq_ready, c + 1)
                wait(pe, s_out_ready, c - 1)
                for tt in range(TT):
                    for k in range(KT):
                        last = mm(tok_tile(tt), xq[:, k * CH + tt * P:k * CH + (tt + 1) * P],
                                  tok_wq[:, k * D:(k + 1) * D], start=(k == 0), stop=(k == KT - 1))
                last.then_inc(s_conv_done, 1)

            def turn1(c):
                turn(c, 0, [(s_eg_ready, (c - 1) * EX)])

            def in_x(c):
                pe.wait_ge(s_xt1a, c + 1)
                pe.wait_ge(s_xt1b, c + 1)
                pe.wait_ge(s_h0_ready, c + 1)
                project(F[2], F[3][:, 0:HALF], in_w, 0, xt[0][:], xtr[0][:]).then_inc(s_px_done, 1)

            def in_z(c):
                project(F[0], F[1][:, 0:HALF], in_w, D, xt[0][:], xtr[0][:]).then_inc(s_pz_done, 1)

            def delta_bc(c):
                pe.wait_ge(s_xc_ready, c + 1)
                pe.wait_ge(s_zt_ready, c + 1)
                pe.wait_ge(s_zh_ready, c + 1)
                pe.wait_ge(s_cv0_ready, c + 1)
                pe.wait_ge(s_xin_ready, c + 1)
                x = xc[c_par[0]]
                mm(F[2][0:96, :], bc_w[:, 0, :], x[:, A], start=True, stop=True)
                remainder(F[2][0:96, :], bc_w[:, 1, :], x, 0)
                mm(F[0], delta_w[:, 0, 0:P], x[:, A], start=True, stop=True)
                remainder(F[0], delta_w[:, 1, 0:P], x, 0).then_inc(s_lower_rows, 1)
                for rows, toks in halves:
                    mm(F[1][rows, 0:HALF], delta_w[:, 0, P:D], x[:, toks], start=True, stop=False)
                    mm(F[1][rows, 0:HALF], delta_w[rows, 1, P:D], x[rows, B], start=False, stop=True)
                pe.wait_ge(s_lower_rows, c + 1)
                remainder(F[0], delta_w[:, 1, 0:P], x, 1).then_inc(s_pd_done, 1)
                remainder(F[2][0:96, :], bc_w[:, 1, :], x, 1).then_inc(s_pbc_done, 1)

            def spread(c, par, u):
                kind, n = UNITS[u]
                if u == 0:
                    pe.wait_ge(s_bc_ready, c + 1)
                for dst, row, free, sem in ((pb, n, s_h_ready, s_b_spread), (pc, N + n, s_c_copied, s_c_spread)):
                    wait(pe, free, c * NU + u)
                    if kind == "A":
                        last = mm(dst[:], sel[:, row, :], bc[par][:, :], start=True, stop=True)
                    else:
                        for j in range(2):
                            for rows, toks in halves:
                                last = mm(dst[rows, j * HALF:(j + 1) * HALF], sel[:, row + j, 0:64],
                                          bc[par][:, toks], start=True, stop=True)
                    last.then_inc(sem, 1)

            def add_y(c, u):
                kind, n = UNITS[u]
                pe.wait_ge(s_hc_ready, c * NU + u + 1)
                if u == 0:
                    wait(pe, s_ys_ready, c)
                src = hc[u % Y_RING]
                if kind == "A":
                    mm(py[:, 0, :], ident[:], src[:], start=(n == 0), stop=(n == N - 1),
                       skip_group_check=True).then_inc(s_y_added, 1)
                else:
                    mm(py[:, 1, 0:HALF], ident[:], src[:, 0:HALF], start=(n == 0), stop=False,
                       skip_group_check=True)
                    mm(py[:, 1, 0:HALF], ident[:], src[:, HALF:CH], start=False, stop=(n == N - 2),
                       skip_group_check=True).then_inc(s_y_added, 1)

            def out_proj(c):
                pe.wait_ge(s_yg_ready, c + 1)
                if c_next[0]:
                    pe.wait_ge(s_bc_r, c + 2)
                    pe.wait_ge(s_bc_hi, c + 2)
                for tt in range(TT):
                    rows = halves[tt // 2][0]
                    b0 = CH + (tt % 2) * P
                    mm(tok_tile(tt), yg[:, tt * P:(tt + 1) * P], out_w[:, 0, :], start=True, stop=False)
                    last = mm(tok_tile(tt), yg[rows, b0:b0 + P], out_w[rows, 1, :], start=False, stop=True)
                last.then_inc(s_po_done, 1)

            def turn2(c):
                turn(c, 1, [(s_relu_ready, c + 2), (s_abs_ready, c + 2)] if c_next[0] else [])

            def gate(c):
                pe.wait_ge(s_xt2a, c + 1)
                pe.wait_ge(s_xt2b, c + 1)
                pe.wait_ge(s_h1_ready, c + 1)
                for tt in range(TT):
                    dst = F[3][:, tt * E:(tt + 1) * E]
                    mm(dst, xt[1][:, tt * P:(tt + 1) * P], gate_w[:, 0, :], start=True, stop=False)
                    last = mm(dst, xtr[1][:, tt * P:(tt + 1) * P], gate_w[0:DR, 1, :], start=False, stop=True)
                last.then_inc(s_pg_done, 1)

            def turn_cw(c):
                pe.wait_ge(s_cw_ready, c + 1)
                for tt in range(TT):
                    last = nc.tensor.transpose(pc_free(tt), cw3[:, tt, :, :].rearrange("p a b -> p (a b)"), ident[:])
                last.then_inc(s_cwt_done, 1)

            def pc_free(tt):
                return F[3][0:96, tt * P:(tt + 1) * P]

            def spread_cw(c, e):
                if e == 0:
                    pe.wait_ge(s_cw_parts, c + 1)
                wait(pe, s_eg_ready, c * EX + 1)
                if e >= 2:
                    pe.wait_ge(s_cw_copied, c * E + e - 1)
                mm(F[e % 2], sel[:, e, :], cws[:, :], start=True, stop=True).then_inc(s_cw_spread, 1)

            def expert_up(c, k):
                e = E if k == 0 else k - 1
                if k == 1:
                    pe.wait_ge(s_cw_copied, (c + 1) * E)
                if k >= 2:
                    pe.wait_ge(s_eg_ready, c * EX + k)
                for dst, w, sem in ((F[0], w1, s_e1_done), (F[1], w3, s_e3_done)):
                    mm(dst, w[:, 0, e, :], xt[1][:], start=True, stop=False)
                    mm(dst, w[0:DR, 1, e, :], xtr[1][:], start=False, stop=True).then_inc(sem, 1)

            def expert_down(c, k):
                e = E if k == 0 else k - 1
                if k == 0:
                    pe.wait_ge(s_cw_r, c + 1)
                    pe.wait_ge(s_cw_hi, c + 1)
                if k == 0:
                    pe.wait_ge(s_eg_ready, c * EX + 1)
                else:
                    pe.wait_ge(s_eh_ready, c * E + k)
                for tt in range(TT):
                    last = mm(tok_tile(tt), eh[k % 2][:, tt * P:(tt + 1) * P], w2[:, e, :],
                              start=(k == 0 and tt % 2 == 0), stop=(k == EX - 1), skip_group_check=True)
                last.then_inc(s_e2_done, 1)

            c_par, c_next = [0], [True]

            def misc(slot, i, post, pre):
                if post:
                    c = i - 1
                    if slot == 0:
                        out_proj(c)
                    if slot == 2:
                        turn2(c)
                    if slot == 3:
                        gate(c)
                        expert_up(c, 0)
                    if slot == 6:
                        turn_cw(c)
                    if slot == 7:
                        for e in range(E):
                            spread_cw(c, e)
                        expert_up(c, 1)
                        expert_down(c, 0)
                    if 8 <= slot < 15:
                        expert_up(c, slot - 6)
                        expert_down(c, slot - 7)
                    if slot == 15:
                        expert_down(c, 8)
                if pre:
                    c = i + 1
                    if slot == 16:
                        embed(c)
                    if slot == 18:
                        turn1(c)
                    if slot == 19:
                        in_x(c)
                    if slot == 20:
                        in_z(c)
                    if slot == 22:
                        delta_bc(c)

            def body(i, par, post=True, pre=True):
                c_par[0] = 1 - par
                c_next[0] = True
                for u in range(NU):
                    spread(i, par, u)
                    if u >= 2:
                        add_y(i, u - 2)
                    misc(u, i, post, pre)
                add_y(i, NU - 2)
                add_y(i, NU - 1)

            pe.wait_ge(s_prep, 1)
            c_par[0] = 0
            embed(0)
            turn1(0)
            in_x(0)
            in_z(0)
            delta_bc(0)
            over_chunks(pe, lambda: body(0, 0, post=False), body, lambda: body(n_chunks - 1, 1, pre=False))
            c_next[0] = False
            for slot in range(NU):
                misc(slot, n_chunks, True, False)

        @block.scalar
        def _(act):
            f = nc.scalar.activation

            def scale_x(c):
                act.wait_ge(s_x_in, (c + 1) * 16)
                f(xs[:], xs[:], ACT.Identity, bias=round_col[:], scale=inv_alpha[:, 0:1]).then_inc(s_x_scaled, 1)

            def copy_turned(c, i):
                act.wait_ge([s_tr1, s_tr2][i], c + 1)
                f(xt[i][:], F[0], ACT.Copy).then_inc([s_xt1a, s_xt2a][i], 1)

            def x_evac(c):
                act.wait_ge(s_px_done, c + 1)
                wait(act, s_cv2_ready, c * 2)
                for part, (dst, src) in enumerate(((A, F[2]), (B, F[3][:, 0:HALF]))):
                    last = f(xin[:, dst], src, ACT.Identity, bias=col(cols, "in_b_x", part))
                last.then_inc(s_xin_ready, 1)
                wait(act, s_xc_ready, c)
                for part, (dst, src) in enumerate(((A, F[2]), (B, F[3][:, 0:HALF]))):
                    last = f(cv[:, dst], src, ACT.Identity, bias=conv_bias[:, part:part + 1],
                             scale=col(col_half, "conv_w1", part))
                last.then_inc(s_cv0_ready, 1)

            def z_evac(c):
                act.wait_ge(s_pz_done, c + 1)
                wait(act, s_zs_ready, c)
                srcs = ((A, F[0]), (B, F[1][:, 0:HALF]))
                for part, (dst, src) in enumerate(srcs):
                    last = f(zh[:, dst], src, ACT.Identity, bias=col(col_half, "in_b_z", part), scale=0.5)
                last.then_inc(s_zh_ready, 1)
                for part, (dst, src) in enumerate(srcs):
                    last = f(zt[:, dst], src, ACT.Tanh, bias=col(col_half, "in_b_z", part), scale=0.5)
                last.then_inc(s_zt_ready, 1)

            def conv_tanh(c):
                act.wait_ge(s_cv2_ready, (c + 1) * 2)
                f(cvt[:], cv[:], ACT.Tanh).then_inc(s_cvt_ready, 1)

            def softplus(c):
                act.wait_ge(s_pd_done, c + 1)
                srcs = ((A, F[0]), (B, F[1][:, 0:HALF]))
                wait(act, s_dt_ready, c)
                for part, (dst, src) in enumerate(srcs):
                    last = f(sp_relu[:, dst], src, ACT.Relu, bias=col(cols, "delta_b", part))
                last.then_inc(s_relu_ready, 1)
                for part, (dst, src) in enumerate(srcs):
                    last = f(sp_ln[:, dst], src, ACT.Abs, bias=col(cols, "delta_b", part))
                last.then_inc(s_abs_ready, 1)
                act.wait_ge(s_abs_ready, c + 1)
                f(sp_ln[:], sp_ln[:], ACT.Exp, scale=-1.0).then_inc(s_spe_ready, 1)
                act.wait_ge(s_spe_ready, c + 1)
                f(sp_ln[:], sp_ln[:], ACT.Ln, bias=1.0).then_inc(s_spl_ready, 1)

            def bc_high(c, par):
                act.wait_ge(s_pbc_done, c + 1)
                wait(act, s_c_spread, (c - 1) * NU)
                f(bc[par][:, :], F[2][0:96, :], ACT.Copy).then_inc(s_bc_hi, 1)

            def decays(c, par, u):
                kind, n = UNITS[u]
                if u == 0:
                    act.wait_ge(s_dt_ready, c + 1)
                wait(act, s_h_ready, c * NU + u - A_RING + 1)
                dst = images(decay[u % A_RING][:])
                src = images(dt[par][:])
                if kind == "A":
                    f(dst[:, :, 1:L], src[:, 0:8, 1:L], ACT.Exp, scale=a_neg[:, n:n + 1]).then_inc(s_decay_ready, 1)
                else:
                    for j in range(2):
                        last = f(dst[:, 4 * j:4 * j + 4, 1:L], src[:, 8:12, 1:L], ACT.Exp,
                                 scale=a_neg[:, N + n + j:N + n + j + 1])
                    last.then_inc(s_decay_ready, 1)

            def copy_c(c, u):
                act.wait_ge(s_c_spread, c * NU + u + 1)
                wait(act, s_hc_ready, c * NU + u - C_RING + 1)
                f(cs[u % C_RING][:], pc[:], ACT.Copy).then_inc(s_c_copied, 1)

            def gate_tanh(c):
                act.wait_ge(s_pg_done, c + 1)
                f(gt[:], F[3][:, 0:TT * E], ACT.Tanh, scale=0.5).then_inc(s_gt_ready, 1)

            def cw_high(c):
                act.wait_ge(s_cwt_done, c + 1)
                f(cws[:, :], F[3][0:96, :], ACT.Copy).then_inc(s_cw_hi, 1)

            def copy_cw(c, e):
                act.wait_ge(s_cw_spread, c * E + e + 1)
                f(cwr[:, e, :], F[e % 2], ACT.Copy).then_inc(s_cw_copied, 1)

            def expert_tanh(c, k):
                act.wait_ge(s_e1_done, c * EX + k + 1)
                if k:
                    act.wait_ge(s_eq_ready, c * EX + k)
                f(et[:], F[0], ACT.Tanh, scale=0.5).then_inc(s_et_ready, 1)

            def misc(slot, i, par, post, pre):
                if post:
                    c = i - 1
                    if slot == 2:
                        copy_turned(c, 1)
                    if slot == 3:
                        gate_tanh(c)
                        expert_tanh(c, 0)
                    if slot == 6:
                        cw_high(c)
                    if slot == 7:
                        for e in range(E):
                            copy_cw(c, e)
                        expert_tanh(c, 1)
                    if 8 <= slot < 15:
                        expert_tanh(c, slot - 6)
                if pre:
                    c = i + 1
                    if slot == 10:
                        scale_x(c)
                    if slot == 18:
                        copy_turned(c, 0)
                    if slot == 19:
                        x_evac(c)
                    if slot == 20:
                        conv_tanh(c)
                        z_evac(c)
                    if slot == 22:
                        softplus(c)
                        bc_high(c, 1 - par)

            def body(i, par, post=True, pre=True):
                for u in range(NU):
                    decays(i, par, u)
                    copy_c(i, u)
                    misc(u, i, par, post, pre)

            act.wait_ge(s_w_in, W_ALL)
            f(a_neg[:], a_log[:], ACT.Exp).then_inc(s_avec_exp, 1)
            act.wait_ge(s_cols_ready, 1)
            f(tok_w, tok_w, ACT.Identity, bias=round_col[:], scale=inv_alpha[:, 1:2]).then_inc(s_tokw_scaled, 1)
            act.wait_ge(s_prep, 1)
            scale_x(0)
            copy_turned(0, 0)
            x_evac(0)
            conv_tanh(0)
            z_evac(0)
            softplus(0)
            bc_high(0, 0)
            over_chunks(act, lambda: body(0, 0, post=False), body, lambda: body(n_chunks - 1, 1, pre=False))
            for slot in range(NU):
                misc(slot, n_chunks, 0, True, False)

        @block.vector
        def _(dve):
            v = nc.vector

            def quantise(c):
                dve.wait_ge(s_x_scaled, c + 1)
                wait(dve, s_conv_done, c)
                v.tensor_scalar(xq[:], xs[:], ROUND, 127.0, ALU.subtract, ALU.min).then_inc(s_xq_top, 1)
                dve.wait_ge(s_xq_top, c + 1)
                v.tensor_scalar(xq[:], xq[:], -128.0, None, ALU.max).then_inc(s_xq_ready, 1)

            def embed_out(c, par):
                dve.wait_ge(s_conv_done, c + 1)
                wait(dve, s_h0b_ready, c - 1)
                for i in range(2):
                    dst = h0[par][:, 2 * i:2 * i + 2, :].rearrange("p t d -> p (t d)")
                    last = v.scalar_tensor_tensor(dst, F[2 + i][:, 0:2 * D], alpha_prod[:, 0:1], tok_b[:],
                                                  ALU.mult, ALU.add)
                last.then_inc(s_h0_ready, 1)

            def norm_stats(c, i, src, src_sem):
                st_sem, mv_sem, ve_sem = [(s_st1, s_mv1, s_ve1), (s_st2, s_mv2, s_ve2)][i]
                dve.wait_ge(src_sem, c + 1)
                for tt in range(TT):
                    last = v.bn_stats(stats[i][:, tt, :], src[:, tt, :])
                last.then_inc(st_sem, 1)
                dve.wait_ge(st_sem, c + 1)
                dve.sem_inc(s_stats_seen, 1)
                for tt in range(TT):
                    last = v.bn_aggr(mv[i][:, tt, :], stats[i][:, tt, :])
                last.then_inc(mv_sem, 1)
                dve.wait_ge(mv_sem, c + 1)
                v.tensor_scalar(vare[i][:], mv[i][:, :, 1], LN_EPS, None, ALU.add).then_inc(ve_sem, 1)

            def norm_apply(c, i, src):
                dve.wait_ge([s_mv1, s_mv2][i], c + 1)
                dve.wait_ge([s_rs1, s_rs2][i], c + 1)
                for tt in range(TT):
                    last = v.tensor_scalar(xn[i][:, tt, :], src[:, tt, :], mv[i][:, tt, 0:1],
                                           rstd[i][:, tt:tt + 1], ALU.subtract, ALU.mult)
                last.then_inc([s_xn1, s_xn2][i], 1)

            def copy_turned(c, i):
                dve.wait_ge([s_tr1, s_tr2][i], c + 1)
                v.tensor_copy(xtr[i][:], F[1][0:DR, :]).then_inc([s_xt1b, s_xt2b][i], 1)

            def conv(c):
                dve.wait_ge(s_xin_ready, c + 1)
                dve.wait_ge(s_cv0_ready, c + 1)
                for name, dst_l, src_l, done in (("conv_w0", slice(1, L), slice(0, L - 1), s_cv1_ready),
                                                 ("conv_w2", slice(0, L - 1), slice(1, L), s_cv2_ready)):
                    for part, cols_ in enumerate((A, B)):
                        o = images(cv[:, cols_])[:, :, dst_l]
                        ins = v.scalar_tensor_tensor(o, images(xin[:, cols_])[:, :, src_l],
                                                     col(col_half, name, part), o, ALU.mult, ALU.add)
                        ins.then_inc(done, 1)
                    if done is s_cv1_ready:
                        dve.wait_ge(s_cv1_ready, (c + 1) * 2)

            def conv_gate(c, par):
                dve.wait_ge(s_cvt_ready, c + 1)
                wait(dve, s_ys_ready, c - 1)
                v.scalar_tensor_tensor(xc[par][:], cvt[:], 1.0, cv[:], ALU.add, ALU.mult).then_inc(s_xc_ready, 1)

            def z_gate(c, par):
                dve.wait_ge(s_zt_ready, c + 1)
                dve.wait_ge(s_zh_ready, c + 1)
                wait(dve, s_yg_ready, c - 1)
                v.scalar_tensor_tensor(zs[par][:], zt[:], 1.0, zh[:], ALU.add, ALU.mult).then_inc(s_zs_ready, 1)

            def split(c, src, hi, r, m, sems):
                hi_sem, r_sem, m_sem, mid_sem, done = sems
                dve.wait_ge(hi_sem, c + 1)
                v.tensor_tensor(r[:], src, hi[:], ALU.subtract).then_inc(r_sem, 1)
                dve.wait_ge(r_sem, c + 1)
                v.tensor_copy(m[:], r[:]).then_inc(m_sem, 1)
                dve.wait_ge(m_sem, c + 1)
                v.tensor_copy(hi[32:64, :], m[32:64, :]).then_inc(mid_sem, 1)
                dve.wait_ge(mid_sem, c + 1)
                v.tensor_tensor(hi[64:96, :], r[64:96, :], m[64:96, :], ALU.subtract).then_inc(done, 1)

            def split_bc(c, par):
                split(c, F[2][0:96, :], bc[par], split_r, split_m, (s_bc_hi, s_bc_r, s_bc_m, s_bc_mid, s_bc_ready))

            def split_cw(c):
                dve.wait_ge(s_eg_ready, c * EX + 1)
                split(c, F[3][0:96, :], cws, csplit_r, csplit_m, (s_cw_hi, s_cw_r, s_cw_m, s_cw_mid, s_cw_parts))

            def step_sizes(c, par):
                dve.wait_ge(s_relu_ready, c + 1)
                dve.wait_ge(s_spl_ready, c + 1)
                wait(dve, s_decay_ready, (c - 1) * NU)
                v.tensor_tensor(dt[par][:], sp_relu[:], sp_ln[:], ALU.add).then_inc(s_dt_ready, 1)
                dve.wait_ge(s_dt_ready, c + 1)
                wait(dve, s_b_times_u, (c - 1) * NU)
                v.tensor_tensor(ut[par][:], dt[par][:], xc[par][:], ALU.mult).then_inc(s_ut_ready, 1)

            def scan(c, par, u):
                kind, n = UNITS[u]
                if u == 0:
                    dve.wait_ge(s_ut_ready, c + 1)
                dve.wait_ge(s_b_spread, c * NU + u + 1)
                if kind == "A":
                    v.tensor_tensor(pb[:], pb[:], ut[par][:, A], ALU.mult).then_inc(s_b_times_u, 1)
                else:
                    two = pb[:].rearrange("p (j m) -> p j m", j=2)
                    v.tensor_tensor(two, two, ut[par][:, B].unsqueeze(1).broadcast_to([P, 2, HALF]),
                                    ALU.mult).then_inc(s_b_times_u, 1)
                dve.wait_ge(s_decay_ready, c * NU + u + 1)
                wait(dve, s_hc_ready, c * NU + u - H_RING + 1)
                dve.wait_ge(s_b_times_u, c * NU + u + 1)
                v.tensor_tensor_scan(hs[u % H_RING][:], decay[u % A_RING][:], pb[:], 0.0,
                                     ALU.mult, ALU.add).then_inc(s_h_ready, 1)

            def mixer_out(c, par):
                dve.wait_ge(s_y_added, (c + 1) * NU)
                for part, (cols_, src) in enumerate(((A, py[:, 0, :]), (B, py[:, 1, 0:HALF]))):
                    last = v.scalar_tensor_tensor(ys[:, cols_], xc[par][:, cols_], col(cols, "D_param", part), src,
                                                  ALU.mult, ALU.add)
                last.then_inc(s_ys_ready, 1)
                dve.wait_ge(s_ys_ready, c + 1)
                v.tensor_tensor(yg[:], ys[:], zs[par][:], ALU.mult).then_inc(s_yg_ready, 1)

            def residual(c):
                dve.wait_ge(s_po_done, c + 1)
                dve.wait_ge(s_h0b_ready, c + 1)
                dve.wait_ge(s_out_stored, c * 16 + 1)
                for i in range(2):
                    last = v.tensor_tensor(h1[:, 2 * i:2 * i + 2, :], bank_pair(i), h0b[:, 2 * i:2 * i + 2, :], ALU.add)
                last.then_inc(s_h1_ready, 1)

            def beats(c, gt_, ge_, values, n, before, sems, keep=None):
                gt_sem, ge_sem, m_sem = sems
                other = values.unsqueeze(2).broadcast_to([P, TT, n, n])
                own = values.unsqueeze(3).broadcast_to([P, TT, n, n])
                lower = before[:].rearrange("p (a b) -> p a b", a=n).unsqueeze(1).broadcast_to([P, TT, n, n])
                v.tensor_tensor(gt_[:], other, own, ALU.is_gt).then_inc(gt_sem, 1)
                v.tensor_tensor(ge_[:], other, own, ALU.is_ge).then_inc(ge_sem, 1)
                dve.wait_ge(ge_sem, 2 * c + 1)
                v.tensor_tensor(ge_[:], ge_[:], lower, ALU.mult).then_inc(ge_sem, 1)
                dve.wait_ge(ge_sem, 2 * c + 2)
                dve.wait_ge(gt_sem, c + 1)
                v.tensor_tensor(gt_[:], gt_[:], ge_[:], ALU.max).then_inc(m_sem, 1)
                dve.wait_ge(m_sem, c + 1)

            def route(c):
                dve.wait_ge(s_gt_ready, c + 1)
                v.tensor_scalar(score[:].rearrange("p t e -> p (t e)"), gt[:], 0.5, 0.5, ALU.mult,
                                ALU.add).then_inc(s_score_ready, 1)
                dve.wait_ge(s_score_ready, c + 1)
                v.tensor_tensor(biased[:], score[:], gate_b[:].rearrange("p (t e) -> p t e", e=E),
                                ALU.add).then_inc(s_biased_ready, 1)
                dve.wait_ge(s_biased_ready, c + 1)
                pairs = biased[:].rearrange("p t (g j) -> p t g j", j=2)
                v.tensor_tensor(gsum[:], pairs[:, :, :, 0], pairs[:, :, :, 1], ALU.add).then_inc(s_gsum_ready, 1)
                dve.wait_ge(s_gsum_ready, c + 1)
                beats(c, g_gt, g_ge, gsum[:], 4, before4, (s_ggt_ready, s_gge_ready, s_gm_ready))
                v.tensor_reduce(g_rank[:], g_gt[:], AX.X, ALU.add).then_inc(s_grank_ready, 1)
                dve.wait_ge(s_grank_ready, c + 1)
                v.tensor_scalar(g_sel[:], g_rank[:], 2.0, None, ALU.is_lt).then_inc(s_gsel_ready, 1)
                dve.wait_ge(s_gsel_ready, c + 1)
                beats(c, e_gt, e_ge, biased[:], 8, before8, (s_egt_ready, s_ege_ready, s_em_ready))
                sel_b = g_sel[:].unsqueeze(3).broadcast_to([P, TT, 4, 2])
                v.tensor_copy(e_sel[:].rearrange("p t (g j) -> p t g j", j=2), sel_b).then_inc(s_esel_ready, 1)
                dve.wait_ge(s_esel_ready, c + 1)
                v.tensor_tensor(e_gt[:], e_gt[:], e_sel[:].unsqueeze(2).broadcast_to([P, TT, 8, 8]),
                                ALU.mult).then_inc(s_ems_ready, 1)
                dve.wait_ge(s_ems_ready, c + 1)
                v.tensor_reduce(e_rank[:], e_gt[:], AX.X, ALU.add).then_inc(s_erank_ready, 1)
                dve.wait_ge(s_erank_ready, c + 1)
                v.scalar_tensor_tensor(e_sel[:], e_rank[:], 2.0, e_sel[:], ALU.is_lt, ALU.mult)\
                    .then_inc(s_esel2_ready, 1)
                dve.wait_ge(s_esel2_ready, c + 1)
                v.tensor_tensor(e_w[:], e_sel[:], score[:], ALU.mult).then_inc(s_ew_ready, 1)
                dve.wait_ge(s_ew_ready, c + 1)
                v.tensor_reduce(wsum[:], e_w[:], AX.X, ALU.add).then_inc(s_wsum_ready, 1)
                dve.wait_ge(s_wsum_ready, c + 1)
                v.tensor_scalar(wsum[:], wsum[:], 1e-6, None, ALU.add).then_inc(s_weps_ready, 1)
                dve.wait_ge(s_weps_ready, c + 1)
                v.reciprocal(winv[:], wsum[:]).then_inc(s_winv_ready, 1)
                dve.wait_ge(s_winv_ready, c + 1)
                for copy in range(3):
                    last = v.tensor_tensor(cw3[:, :, copy, 0:E], e_w[:], winv[:].unsqueeze(2).broadcast_to([P, TT, E]),
                                           ALU.mult)
                last.then_inc(s_cw_ready, 1)

            def expert_mul(c, k):
                dve.wait_ge(s_et_ready, c * EX + k + 1)
                if k:
                    dve.wait_ge(s_eg_ready, c * EX + k)
                if k == 1:
                    dve.wait_ge(s_cw_parts, c + 1)
                v.scalar_tensor_tensor(eq[:], et[:], 1.0, F[0], ALU.add, ALU.mult).then_inc(s_eq_ready, 1)
                dve.wait_ge(s_e3_done, c * EX + k + 1)
                dve.wait_ge(s_eq_ready, c * EX + k + 1)
                if k >= 3:
                    dve.wait_ge(s_eh_ready, c * E + k - 2)
                v.tensor_tensor(eg[k % 2][:] if k else eh[0][:], eq[:], F[1], ALU.mult).then_inc(s_eg_ready, 1)

            def finish(c):
                dve.wait_ge(s_e2_done, (c + 1) * EX)
                for i in range(2):
                    last = v.tensor_tensor(h1[:, 2 * i:2 * i + 2, :], bank_pair(i), h1[:, 2 * i:2 * i + 2, :], ALU.add)
                last.then_inc(s_out_ready, 1)

            def misc(slot, i, par, post, pre):
                if post:
                    c = i - 1
                    if slot == 1:
                        residual(c)
                        norm_stats(c, 1, h1, s_h1_ready)
                    if slot == 2:
                        norm_apply(c, 1, h1)
                        copy_turned(c, 1)
                    if slot == 4:
                        expert_mul(c, 0)
                        route(c)
                    if slot == 6:
                        split_cw(c)
                    if 7 <= slot < 15:
                        expert_mul(c, slot - 6)
                    if slot == 15:
                        finish(c)
                if pre:
                    c = i + 1
                    if slot == 11:
                        quantise(c)
                    if slot == 17:
                        embed_out(c, 1 - par)
                        norm_stats(c, 0, h0[1 - par], s_h0_ready)
                    if slot == 18:
                        norm_apply(c, 0, h0[1 - par])
                        copy_turned(c, 0)
                    if slot == 20:
                        conv(c)
                    if slot == 21:
                        conv_gate(c, 1 - par)
                        z_gate(c, 1 - par)
                    if slot == 23:
                        split_bc(c, 1 - par)
                        step_sizes(c, 1 - par)

            def body(i, par, post=True, pre=True):
                if post:
                    mixer_out(i - 1, 1 - par)
                for u in range(NU):
                    scan(i, par, u)
                    misc(u, i, par, post, pre)

            v.memset(round_col[:], ROUND)
            v.memset(neg_half[:], -0.5)
            v.memset(cw3[:].rearrange("p a b c -> p (a b c)"), 0.0)
            for i in range(A_RING):
                v.memset(decay[i][:], 0.0)
            dve.wait_ge(s_w_in, W_ALL)
            v.reciprocal(inv_alpha[:], alphas[:])
            v.tensor_tensor(alpha_prod[:], alphas[:, 0:1], alphas[:, 1:2], ALU.mult)
            v.tensor_scalar(col_half[:], cols[:], 0.5, None, ALU.mult)
            v.tensor_scalar(w2[:], w2[:], 0.5, None, ALU.mult).then_inc(s_cols_ready, 1)
            dve.wait_ge(s_cols_ready, 1)
            ib, cw1, cb = (2 * COLS.index(n) for n in ("in_b_x", "conv_w1", "conv_b"))
            v.tensor_tensor(conv_bias[:], cols[:, ib:ib + 2], col_half[:, cw1:cw1 + 2], ALU.mult).then_inc(s_consts, 1)
            dve.wait_ge(s_consts, 1)
            v.tensor_tensor(conv_bias[:], conv_bias[:], col_half[:, cb:cb + 2], ALU.add).then_inc(s_consts, 1)
            dve.wait_ge(s_avec_exp, 1)
            v.tensor_scalar(a_neg[:], a_neg[:], -1.0, None, ALU.mult).then_inc(s_avec_ready, 1)
            dve.wait_ge(s_tokw_scaled, 1)
            v.tensor_scalar(tok_w, tok_w, ROUND, 127.0, ALU.subtract, ALU.min).then_inc(s_tokw_clamped, 1)
            dve.wait_ge(s_tokw_clamped, 1)
            dve.wait_ge(s_avec_ready, 1)
            dve.wait_ge(s_consts, 2)
            v.tensor_scalar(tok_wq[:], tok_w, -128.0, None, ALU.max).then_inc(s_prep, 1)

            quantise(0)
            embed_out(0, 0)
            norm_stats(0, 0, h0[0], s_h0_ready)
            norm_apply(0, 0, h0[0])
            copy_turned(0, 0)
            conv(0)
            conv_gate(0, 0)
            z_gate(0, 0)
            split_bc(0, 0)
            step_sizes(0, 0)
            over_chunks(dve, lambda: body(0, 0, post=False), body, lambda: body(n_chunks - 1, 1, pre=False))
            mixer_out(n_chunks - 1, 1)
            for slot in range(NU):
                misc(slot, n_chunks, 0, True, False)

        @block.gpsimd
        def _(pool):
            g = nc.gpsimd

            def inv_std(c, i):
                ve_sem, rs_sem = [(s_ve1, s_rs1), (s_ve2, s_rs2)][i]
                pool.wait_ge(ve_sem, c + 1)
                g.tensor_tensor(rstd[i][:], vare[i][:], neg_half[:], ALU.pow).then_inc(rs_sem, 1)

            def with_out_b(c, par):
                pool.wait_ge(s_h0_ready, c + 1)
                flat = "p t d -> p (t d)"
                g.tensor_tensor(h0b[:].rearrange(flat), h0[par][:].rearrange(flat), out_b[:], ALU.add)\
                    .then_inc(s_h0b_ready, 1)

            def times_c(c, u):
                pool.wait_ge(s_h_ready, c * NU + u + 1)
                pool.wait_ge(s_c_copied, c * NU + u + 1)
                wait(pool, s_y_added, c * NU + u - Y_RING + 1)
                g.tensor_tensor(hc[u % Y_RING][:], hs[u % H_RING][:], cs[u % C_RING][:], ALU.mult)\
                    .then_inc(s_hc_ready, 1)

            def expert_weight(c, k):
                pool.wait_ge(s_eg_ready, c * EX + k + 1)
                if k == 1:
                    pool.wait_ge(s_cw_copied, (c + 1) * E)
                if k >= 2:
                    pool.wait_ge(s_e2_done, c * EX + k - 1)
                g.tensor_tensor(eh[k % 2][:], eg[k % 2][:], cwr[:, k - 1, :], ALU.mult).then_inc(s_eh_ready, 1)

            def misc(slot, i, par, post, pre):
                if post:
                    c = i - 1
                    if slot == 0:
                        with_out_b(c, 1 - par)
                    if slot == 1:
                        inv_std(c, 1)
                    if 7 <= slot < 15:
                        expert_weight(c, slot - 6)
                if pre and slot == 17:
                    inv_std(i + 1, 0)

            def body(i, par, post=True, pre=True):
                for u in range(NU):
                    if u >= 1:
                        times_c(i, u - 1)
                    misc(u, i, par, post, pre)
                times_c(i, NU - 1)

            pool.wait_ge(s_prep, 1)
            inv_std(0, 0)
            over_chunks(pool, lambda: body(0, 0, post=False), body, lambda: body(n_chunks - 1, 1, pre=False))
            for slot in range(NU):
                misc(slot, n_chunks, 0, True, False)


def kernel(**inputs):
    import numpy as np
    import ml_dtypes
    import concourse.bacc as bacc
    from concourse.bass_utils import run_bass_kernel_spmd

    a = {k: np.asarray(v) for k, v in inputs.items()}
    f32 = np.float32

    def twice(m):
        return np.stack([m[:P], np.concatenate([m[P:], m[P:]])], axis=1)

    def on_all(v):
        return np.broadcast_to(np.ravel(v), (P, np.size(v)))

    n_img = a["x"].shape[0]
    n_chunks = n_img * L // CH
    x = a["x"].reshape(n_chunks, CH // L, 3, 8, 16, 8, 16).transpose(0, 2, 4, 6, 1, 3, 5)
    x = x.reshape(n_chunks, KT, P, CH).transpose(0, 2, 1, 3).reshape(n_chunks, P, KT * CH)
    tok_w = a["L0_tok_W"].reshape(D, KT, P).transpose(2, 1, 0).reshape(P, KT * D)
    in_b, conv_w = a["L0_attn_in_b"], a["L0_attn_conv_w"]
    vectors = [in_b[:D], in_b[D:], conv_w[:, 0, 0], conv_w[:, 0, 1], conv_w[:, 0, 2],
               a["L0_attn_conv_b"], a["L0_attn_delta_b"], a["L0_attn_D_param"]]
    bc_w = np.concatenate([a["L0_attn_B_proj_w"], a["L0_attn_C_proj_w"]] * 3).T
    w1 = np.concatenate([a["L0_ffn_w1"], a["L0_ffn_sw1"][None]])
    w3 = np.concatenate([a["L0_ffn_w3"], a["L0_ffn_sw3"][None]])
    w2 = np.concatenate([a["L0_ffn_w2"], a["L0_ffn_sw2"][None]])
    sel = np.zeros((96, 2 * N, P), ml_dtypes.bfloat16)
    for part in range(3):
        for r in range(2 * N):
            sel[32 * part + r, r, :] = 1
    laid = {
        "x": x, "ident": np.eye(P, dtype=f32), "sel": sel,
        "cols": np.stack([twice(v) for v in vectors], axis=1).reshape(P, NCOL),
        "alphas": on_all(np.stack([a["L0_tok_alpha_a"], a["L0_tok_alpha_w"]])),
        "a_log": twice(a["L0_attn_A_log"]).reshape(P, 2 * N),
        "tok_w": tok_w, "tok_b": on_all(np.stack([a["L0_tok_b"]] * 2)),
        "out_b": on_all(np.stack([a["L0_attn_out_b"]] * TT)),
        "in_w": twice(a["L0_attn_in_w"].T), "delta_w": twice(a["L0_attn_delta_w"].T),
        "bc_w": twice(bc_w), "out_w": twice(a["L0_attn_out_w"].T),
        "gate_w": twice(a["L0_ffn_gate_weight"].T), "gate_b": on_all(np.stack([a["L0_ffn_gate_bias"]] * TT)),
        "before4": on_all(np.tril(np.ones((4, 4), f32), -1)), "before8": on_all(np.tril(np.ones((8, 8), f32), -1)),
        "w1": twice(w1.transpose(2, 0, 1)), "w3": twice(w3.transpose(2, 0, 1)), "w2": w2.transpose(2, 0, 1),
    }
    nc = bacc.Bacc("TRN2", target_bir_lowering=False, num_devices=1)
    arrays, aps = {}, {}
    for name, value in laid.items():
        value = np.ascontiguousarray(value)
        arrays[f"in_{name}_dram"] = value
        aps[name] = nc.dram_tensor(f"in_{name}_dram", value.shape, mybir.dt.from_np(value.dtype),
                                   kind="ExternalInput").ap()
    out = nc.dram_tensor("out_0_dram", (n_img, L, D), F32, kind="ExternalOutput").ap()
    out_v = out.rearrange("(c m) l d -> c (m l) d", c=n_chunks).rearrange("c (t p) d -> c p t d", p=P)
    build(nc, aps, out_v)
    got = run_bass_kernel_spmd(nc, [arrays], core_ids=[0])
    return got.results[0]["out_0_dram"]
```

```python
from contextlib import ExitStack

import concourse.bass as bass
from concourse import mybir

F32 = mybir.dt.float32
BF16 = mybir.dt.bfloat16
ALU = mybir.AluOpType
ACT = mybir.ActivationFunctionType
AX = mybir.AxisListType

P = 128
D = 192
DR = D - P
L = 64
CH = 512
HALF = CH // 2
PK = CH + HALF
TT = CH // P
KT = 768 // P
N = 16
E = 8
EX = E + 1
ROUND = 1.5 * 2 ** 23
LN_EPS = 1e-5

UNITS = [u for m in range(0, N, 2) for u in (("A", m), ("A", m + 1), ("B", m))]
NU = len(UNITS)
A_RING, H_RING, C_RING, Y_RING = 3, 3, 2, 3

UP = list(range(14, 14 + EX))
DOWN = [u + 1 for u in UP]
XH = KT * CH // 2

COLS = ["in_b_x", "in_b_z", "conv_w0", "conv_w1", "conv_w2", "conv_b", "delta_b", "D_param"]
NCOL = 2 * len(COLS)


def build(nc, t, out):
    n_chunks = t["x"].shape[0]
    ctx = ExitStack()
    with ctx:
        def sb(name, shape, dt=F32):
            return ctx.enter_context(nc.sbuf_tensor(name, shape, dt))

        ident = sb("ident", [P, P])
        sel = sb("sel", [96, 2 * N, P], BF16)
        cols = sb("cols", [P, NCOL])
        col_half = sb("col_half", [P, NCOL])
        conv_bias = sb("conv_bias", [P, 2])
        alphas = sb("alphas", [P, 2])
        inv_alpha = sb("inv_alpha", [P, 2])
        alpha_prod = sb("alpha_prod", [P, 1])
        round_col = sb("round_col", [P, 1])
        a_log = sb("a_log", [P, 2 * N])
        a_neg = sb("a_neg", [P, 2 * N])
        tok_w = sb("tok_w", [P, KT * D])
        tok_wq = sb("tok_wq", [P, KT * D], BF16)
        tok_b = sb("tok_b", [P, 2 * D])
        out_b = sb("out_b", [P, TT * D])
        in_w = sb("in_w", [P, 2, 2 * D])
        delta_w = sb("delta_w", [P, 2, D])
        bc_w = sb("bc_w", [P, 2, 96])
        out_w = sb("out_w", [P, 2, D])
        gate_w = sb("gate_w", [P, 2, E])
        gate_b = sb("gate_b", [P, TT * E])
        before4 = sb("before4", [P, 16])
        before8 = sb("before8", [P, 64])
        w1 = sb("w1", [P, 2, EX, P])
        w3 = sb("w3", [P, 2, EX, P])
        w2 = sb("w2", [P, EX, D])
        neg_half = sb("neg_half", [P, TT])

        xs = sb("xs", [P, KT * CH])
        xq = sb("xq", [P, KT * CH], BF16)
        h0 = [sb(f"h0_{i}", [P, TT, D]) for i in range(2)]
        h0b = sb("h0b", [P, TT, D])
        stats = [sb(f"stats{i}", [P, TT, 6]) for i in range(2)]
        mv = [sb(f"mv{i}", [P, TT, 2]) for i in range(2)]
        vare = [sb(f"vare{i}", [P, TT]) for i in range(2)]
        rstd = [sb(f"rstd{i}", [P, TT]) for i in range(2)]
        xn = [sb(f"xn{i}", [P, TT, D]) for i in range(2)]
        xt = [sb(f"xt{i}", [P, CH]) for i in range(2)]
        xtr = [sb(f"xtr{i}", [DR, CH]) for i in range(2)]
        xin = sb("xin", [P, PK])
        cv = sb("cv", [P, PK])
        cvt = sb("cvt", [P, PK])
        zh = sb("zh", [P, PK])
        zt = sb("zt", [P, PK])
        sp_relu = sb("sp_relu", [P, PK])
        sp_ln = sb("sp_ln", [P, PK])
        xc = [sb(f"xc{i}", [P, PK]) for i in range(2)]
        zs = [sb(f"zs{i}", [P, PK]) for i in range(2)]
        dt = [sb(f"dt{i}", [P, PK]) for i in range(2)]
        ut = [sb(f"ut{i}", [P, PK]) for i in range(2)]
        bc = [sb(f"bc{i}", [96, CH], BF16) for i in range(2)]
        split_r = sb("split_r", [96, CH])
        split_m = sb("split_m", [96, CH], BF16)
        decay = [sb(f"decay{i}", [P, CH]) for i in range(A_RING)]
        hs = [sb(f"hs{i}", [P, CH]) for i in range(H_RING)]
        cs = [sb(f"cs{i}", [P, CH]) for i in range(C_RING)]
        hc = [sb(f"hc{i}", [P, CH]) for i in range(Y_RING)]
        ya = [sb(f"ya{i}", [P, 2 * CH]) for i in range(2)]
        ys = sb("ys", [P, PK])
        yg = sb("yg", [P, PK])
        h1 = sb("h1", [P, TT, D])
        gt = sb("gt", [P, TT * E])
        score = sb("score", [P, TT, E])
        biased = sb("biased", [P, TT, E])
        gsum = sb("gsum", [P, TT, 4])
        g_gt = sb("g_gt", [P, TT, 4, 4])
        g_ge = sb("g_ge", [P, TT, 4, 4])
        g_rank = sb("g_rank", [P, TT, 4])
        g_sel = sb("g_sel", [P, TT, 4])
        e_gt = sb("e_gt", [P, TT, 8, 8])
        e_ge = sb("e_ge", [P, TT, 8, 8])
        e_rank = sb("e_rank", [P, TT, E])
        e_sel = sb("e_sel", [P, TT, E])
        e_w = sb("e_w", [P, TT, E])
        wsum = sb("wsum", [P, TT])
        winv = sb("winv", [P, TT])
        cw3 = sb("cw3", [P, TT, 3, 32])
        cws = sb("cws", [96, CH], BF16)
        csplit_r = sb("csplit_r", [96, CH])
        csplit_m = sb("csplit_m", [96, CH], BF16)
        cwr = [sb(f"cwr{i}", [P, CH]) for i in range(2)]
        et = sb("et", [P, CH])
        eq = sb("eq", [P, CH])
        eg = [sb(f"eg{i}", [P, CH]) for i in range(2)]
        eh = [sb(f"eh{i}", [P, CH]) for i in range(2)]

        pb = [ctx.enter_context(nc.psum_tensor(f"pb{i}", [P, CH], F32)) for i in range(2)]
        pc = ctx.enter_context(nc.psum_tensor("pc", [P, CH], F32))
        pw = ctx.enter_context(nc.psum_tensor("pw", [P, CH], F32))
        pf = ctx.enter_context(nc.psum_tensor("pf", [P, 4, 512], F32))
        F = [pf[:, i, :] for i in range(4)]

        def sem(name):
            return ctx.enter_context(nc.semaphore(name))

        s_w_in = sem("w_in")
        s_consts = sem("consts")
        s_tokw_scaled = sem("tokw_scaled")
        s_tokw_clamped = sem("tokw_clamped")
        s_tokw_ready = sem("tokw_ready")
        s_avec_exp = sem("avec_exp")
        s_avec_ready = sem("avec_ready")
        s_cols_ready = sem("cols_ready")
        s_prep = sem("prep")
        s_x_in = sem("x_in")
        s_x_scaled = sem("x_scaled")
        s_xq_top = sem("xq_top")
        s_xq_ready = sem("xq_ready")
        s_conv_done = sem("conv_done")
        s_h0_ready = sem("h0_ready")
        s_stats_seen = sem("stats_seen")
        s_st1 = sem("st1")
        s_mv1 = sem("mv1")
        s_ve1 = sem("ve1")
        s_rs1 = sem("rs1")
        s_xn1 = sem("xn1")
        s_tr1 = sem("tr1")
        s_xt1a = sem("xt1a")
        s_xt1b = sem("xt1b")
        s_px_done = sem("px_done")
        s_pz_done = sem("pz_done")
        s_xin_ready = sem("xin_ready")
        s_cv0_ready = sem("cv0_ready")
        s_cv1_ready = sem("cv1_ready")
        s_cv2_ready = sem("cv2_ready")
        s_cvt_ready = sem("cvt_ready")
        s_xc_ready = sem("xc_ready")
        s_zh_ready = sem("zh_ready")
        s_zt_ready = sem("zt_ready")
        s_zs_ready = sem("zs_ready")
        s_lower_rows = sem("lower_rows")
        s_pd_done = sem("pd_done")
        s_pbc_done = sem("pbc_done")
        s_pd_read = sem("pd_read")
        s_relu_ready = sem("relu_ready")
        s_abs_ready = sem("abs_ready")
        s_spe_ready = sem("spe_ready")
        s_spl_ready = sem("spl_ready")
        s_dt_ready = sem("dt_ready")
        s_ut_ready = sem("ut_ready")
        s_bc_hi = sem("bc_hi")
        s_bc_r = sem("bc_r")
        s_bc_m = sem("bc_m")
        s_bc_mid = sem("bc_mid")
        s_bc_ready = sem("bc_ready")
        s_decay_ready = sem("decay_ready")
        s_b_spread = sem("b_spread")
        s_c_spread = sem("c_spread")
        s_b_times_u = sem("b_times_u")
        s_h_ready = sem("h_ready")
        s_c_copied = sem("c_copied")
        s_hc_ready = sem("hc_ready")
        s_y_added = sem("y_added")
        s_yb_ready = sem("yb_ready")
        s_ys_ready = sem("ys_ready")
        s_yg_ready = sem("yg_ready")
        s_po_done = sem("po_done")
        s_h0b_ready = sem("h0b_ready")
        s_h1_ready = sem("h1_ready")
        s_st2 = sem("st2")
        s_mv2 = sem("mv2")
        s_ve2 = sem("ve2")
        s_rs2 = sem("rs2")
        s_xn2 = sem("xn2")
        s_tr2 = sem("tr2")
        s_xt2a = sem("xt2a")
        s_xt2b = sem("xt2b")
        s_pg_done = sem("pg_done")
        s_gt_ready = sem("gt_ready")
        s_score_ready = sem("score_ready")
        s_biased_ready = sem("biased_ready")
        s_gsum_ready = sem("gsum_ready")
        s_ggt_ready = sem("ggt_ready")
        s_gge_ready = sem("gge_ready")
        s_gm_ready = sem("gm_ready")
        s_grank_ready = sem("grank_ready")
        s_gsel_ready = sem("gsel_ready")
        s_egt_ready = sem("egt_ready")
        s_ege_ready = sem("ege_ready")
        s_em_ready = sem("em_ready")
        s_ems_ready = sem("ems_ready")
        s_erank_ready = sem("erank_ready")
        s_esel_ready = sem("esel_ready")
        s_esel2_ready = sem("esel2_ready")
        s_ew_ready = sem("ew_ready")
        s_wsum_ready = sem("wsum_ready")
        s_weps_ready = sem("weps_ready")
        s_winv_ready = sem("winv_ready")
        s_cw_ready = sem("cw_ready")
        s_cwt_done = sem("cwt_done")
        s_cw_hi = sem("cw_hi")
        s_cw_r = sem("cw_r")
        s_cw_m = sem("cw_m")
        s_cw_mid = sem("cw_mid")
        s_cw_parts = sem("cw_parts")
        s_cw_spread = sem("cw_spread")
        s_cw_copied = sem("cw_copied")
        s_e1_done = sem("e1_done")
        s_e3_done = sem("e3_done")
        s_et_ready = sem("et_ready")
        s_eq_ready = sem("eq_ready")
        s_eg_ready = sem("eg_ready")
        s_eh_ready = sem("eh_ready")
        s_e2_done = sem("e2_done")
        s_out_ready = sem("out_ready")
        s_out_stored = sem("out_stored")

        def wait(eng, sem, value):
            if isinstance(value, int) and value <= 0:
                return
            eng.wait_ge(sem, value)

        block = ctx.enter_context(nc.Block())
        A, B = slice(0, CH), slice(CH, PK)
        halves = [(slice(0, 64), slice(0, HALF)), (slice(64, 128), slice(HALF, CH))]

        def col(tile, name, part):
            i = 2 * COLS.index(name) + part
            return tile[:, i:i + 1]

        def added(c, u):
            return c * (NU - 2) + u + 1 - (u >= 0) - (u >= 2)

        def images(ap):
            return ap.rearrange("p (m l) -> p m l", l=L)

        def bank_pair(i):
            return F[2 + i][:, 0:2 * D].rearrange("p (t d) -> p t d", d=D)

        def tok_tile(tt):
            return F[2 + tt // 2][:, (tt % 2) * D:(tt % 2) * D + D]

        WEIGHTS = [(ident, t["ident"]), (sel, t["sel"]), (cols, t["cols"]), (alphas, t["alphas"]), (a_log, t["a_log"]),
                   (tok_w, t["tok_w"]), (tok_b, t["tok_b"]), (out_b, t["out_b"]), (in_w, t["in_w"]),
                   (delta_w, t["delta_w"]), (bc_w, t["bc_w"]), (out_w, t["out_w"]), (gate_w, t["gate_w"]),
                   (gate_b, t["gate_b"]), (before4, t["before4"]), (before8, t["before8"]), (w1, t["w1"]),
                   (w3, t["w3"]), (w2, t["w2"])]
        W_ALL = 16 * len(WEIGHTS)

        def over_chunks(eng, first, middle, last):
            first()
            with eng.Fori(0, (n_chunks - 2) // 2) as k:
                middle(k * 2 + 1, 1)
                middle(k * 2 + 2, 0)
            last()

        @block.sync
        def _(sp):
            for tile, src in WEIGHTS:
                sp.dma_start(tile[:], src).then_inc(s_w_in, 16)

            def load_x(c):
                wait(sp, s_xq_top, 2 * c)
                sp.dma_start(xs[:], t["x"][c]).then_inc(s_x_in, 16)

            def store(c):
                sp.wait_ge(s_out_ready, c + 2)
                sp.dma_start(out[c], h1[:]).then_inc(s_out_stored, 16)

            sp.sem_inc(s_out_stored, 1)
            load_x(0)
            load_x(1)
            load_x(2)
            with sp.Fori(0, n_chunks - 3) as k:
                load_x(k + 3)
                store(k)
            sp.wait_ge(s_x_in, 16 * n_chunks)
            sp.sem_inc(s_x_in, 16)
            for c in range(n_chunks - 3, n_chunks):
                store(c)
            sp.wait_ge(s_out_stored, 16 * n_chunks + 1)

        @block.tensor
        def _(pe):
            mm = nc.tensor.matmul

            def project(dst_a, dst_b, w, m0, rhs_a, rhs_b):
                mm(dst_a, w[:, 0, m0:m0 + P], rhs_a, start=True, stop=False)
                mm(dst_a, w[0:DR, 1, m0:m0 + P], rhs_b, start=False, stop=True)
                for rows, toks in halves:
                    mm(dst_b[rows, :], w[:, 0, m0 + P:m0 + D], rhs_a[:, toks], start=True, stop=False)
                    last = mm(dst_b[rows, :], w[0:DR, 1, m0 + P:m0 + D], rhs_b[:, toks], start=False, stop=True)
                return last

            def remainder(dst, w, rhs, half):
                rows, toks = halves[half]
                return mm(dst[:, toks], w[rows, :], rhs[rows, B], start=False, stop=True,
                          skip_group_check=True)

            def turn(c, i, before):
                pe.wait_ge([s_xn1, s_xn2][i], c + 1)
                for sem, value in before:
                    wait(pe, sem, value)
                for tt in range(TT):
                    nc.tensor.transpose(F[0][:, tt * P:(tt + 1) * P], xn[i][:, tt, 0:P], ident[:])
                for tt in range(TT):
                    last = nc.tensor.transpose(F[1][0:DR, tt * P:(tt + 1) * P], xn[i][:, tt, P:D], ident[:])
                last.then_inc([s_tr1, s_tr2][i], 1)

            def embed(c):
                pe.wait_ge(s_xq_ready, 2 * (c + 1))
                wait(pe, s_out_ready, c - 1)
                wait(pe, s_bc_hi, c)
                wait(pe, s_bc_r, c)
                for tt in range(TT):
                    for k in range(KT):
                        last = mm(tok_tile(tt), xq[:, k * CH + tt * P:k * CH + (tt + 1) * P],
                                  tok_wq[:, k * D:(k + 1) * D], start=(k == 0), stop=(k == KT - 1))
                last.then_inc(s_conv_done, 1)

            def turn1(c):
                turn(c, 0, [(s_pd_read, c)])

            def in_x(c, post):
                pe.wait_ge(s_xt1a, c + 1)
                pe.wait_ge(s_xt1b, c + 1)
                pe.wait_ge(s_h0_ready, c + 1)
                if post:
                    pe.wait_ge(s_h1_ready, c - 1)
                project(F[2], F[3][:, 0:HALF], in_w, 0, xt[0][:], xtr[0][:]).then_inc(s_px_done, 1)

            def in_z(c, post):
                if post:
                    pe.wait_ge(s_xt2a, c - 1)
                    pe.wait_ge(s_xt2b, c - 1)
                project(F[0], F[1][:, 0:HALF], in_w, D, xt[0][:], xtr[0][:]).then_inc(s_pz_done, 1)

            def delta_bc(c, par, step):
                x = xc[par]
                if step == 0:
                    pe.wait_ge(s_xc_ready, c + 1)
                    pe.wait_ge(s_zt_ready, c + 1)
                    pe.wait_ge(s_zh_ready, c + 1)
                    pe.wait_ge(s_cv0_ready, c + 1)
                    pe.wait_ge(s_xin_ready, c + 1)
                    mm(F[2][0:96, :], bc_w[:, 0, :], x[:, A], start=True, stop=True)
                    remainder(F[2][0:96, :], bc_w[:, 1, :], x, 0)
                    mm(F[0], delta_w[:, 0, 0:P], x[:, A], start=True, stop=True)
                    remainder(F[0], delta_w[:, 1, 0:P], x, 0).then_inc(s_lower_rows, 1)
                    return
                for rows, toks in halves:
                    mm(F[1][rows, 0:HALF], delta_w[:, 0, P:D], x[:, toks], start=True, stop=False)
                    mm(F[1][rows, 0:HALF], delta_w[rows, 1, P:D], x[rows, B], start=False, stop=True)
                pe.wait_ge(s_lower_rows, c + 1)
                remainder(F[2][0:96, :], bc_w[:, 1, :], x, 1).then_inc(s_pbc_done, 1)
                remainder(F[0], delta_w[:, 1, 0:P], x, 1).then_inc(s_pd_done, 1)

            def spread(c, par, u):
                kind, n = UNITS[u]
                if u == 0:
                    pe.wait_ge(s_bc_ready, c + 1)
                for dst, row, free, before, sem in ((pb[u % 2], n, s_h_ready, u - 1, s_b_spread),
                                                    (pc, N + n, s_c_copied, u, s_c_spread)):
                    wait(pe, free, c * NU + before)
                    if kind == "A":
                        last = mm(dst[:], sel[:, row, :], bc[par][:, :], start=True, stop=True)
                    else:
                        for j in range(2):
                            for rows, toks in halves:
                                last = mm(dst[rows, j * HALF:(j + 1) * HALF], sel[:, row + j, 0:64],
                                          bc[par][:, toks], start=True, stop=True)
                    last.then_inc(sem, 1)

            def out_proj(c, pre):
                pe.wait_ge(s_yg_ready, c + 1)
                if pre:
                    pe.wait_ge(s_h0_ready, c + 3)
                else:
                    pe.wait_ge(s_out_ready, c + 1)
                for tt in range(TT):
                    rows = halves[tt // 2][0]
                    b0 = CH + (tt % 2) * P
                    mm(tok_tile(tt), yg[:, tt * P:(tt + 1) * P], out_w[:, 0, :], start=True, stop=False)
                    last = mm(tok_tile(tt), yg[rows, b0:b0 + P], out_w[rows, 1, :], start=False, stop=True)
                last.then_inc(s_po_done, 1)

            def turn2(c, pre):
                turn(c, 1, [(s_xt1a, c + 3), (s_xt1b, c + 3)] if pre else [])

            def gate(c):
                pe.wait_ge(s_xt2a, c + 1)
                pe.wait_ge(s_xt2b, c + 1)
                for tt in range(TT):
                    dst = pw[:, tt * E:(tt + 1) * E]
                    mm(dst, xt[1][:, tt * P:(tt + 1) * P], gate_w[:, 0, :], start=True, stop=False)
                    last = mm(dst, xtr[1][:, tt * P:(tt + 1) * P], gate_w[0:DR, 1, :], start=False, stop=True)
                last.then_inc(s_pg_done, 1)

            def turn_cw(c):
                pe.wait_ge(s_cw_ready, c + 1)
                for tt in range(TT):
                    last = nc.tensor.transpose(pw[0:96, tt * P:(tt + 1) * P], cw3[:, tt, :, :].rearrange("p a b -> p (a b)"), ident[:])
                last.then_inc(s_cwt_done, 1)

            def spread_cw(c, e):
                if e == 0:
                    pe.wait_ge(s_cw_parts, c + 1)
                else:
                    pe.wait_ge(s_cw_copied, c * E + e)
                mm(pw[:], sel[:, e, :], cws[:, :], start=True, stop=True).then_inc(s_cw_spread, 1)

            def expert_up(c, k, pre):
                e = E if k == 0 else k - 1
                if k:
                    pe.wait_ge(s_eg_ready, c * EX + k)
                elif pre:
                    pe.wait_ge(s_pd_read, c + 3)
                for dst, w, sem in ((F[0], w1, s_e1_done), (F[1], w3, s_e3_done)):
                    mm(dst, w[:, 0, e, :], xt[1][:], start=True, stop=False)
                    mm(dst, w[0:DR, 1, e, :], xtr[1][:], start=False, stop=True).then_inc(sem, 1)

            def expert_down(c, k, pre):
                e = E if k == 0 else k - 1
                if k == 0 and pre:
                    pe.wait_ge(s_bc_r, c + 3)
                    pe.wait_ge(s_bc_hi, c + 3)
                if k == 0:
                    pe.wait_ge(s_eg_ready, c * EX + 1)
                else:
                    pe.wait_ge(s_eh_ready, c * E + k)
                for tt in range(TT):
                    last = mm(tok_tile(tt), eh[k % 2][:, tt * P:(tt + 1) * P], w2[:, e, :],
                              start=(k == 0 and tt % 2 == 0), stop=(k == EX - 1), skip_group_check=True)
                last.then_inc(s_e2_done, 1)

            def misc(slot, i, par, post, pre):
                if pre:
                    c = i + 1
                    if slot == 0:
                        embed(c)
                    if slot == 4:
                        turn1(c)
                    if slot == 7:
                        in_x(c, post)
                if post:
                    c = i - 1
                    if slot == 3:
                        out_proj(c, pre)
                    if slot == 6:
                        turn2(c, pre)
                    if slot == 8:
                        gate(c)
                if pre:
                    c = i + 1
                    if slot == 8:
                        in_z(c, post)
                    if slot in (11, 12):
                        delta_bc(c, 1 - par, slot - 11)
                if post:
                    c = i - 1
                    if slot == 13:
                        turn_cw(c)
                    for k in range(EX):
                        if slot == UP[k]:
                            expert_up(c, k, pre)
                            if k:
                                spread_cw(c, k - 1)
                    for k in range(EX):
                        if slot == DOWN[k]:
                            expert_down(c, k, pre)

            def body(i, par, post=True, pre=True):
                for u in range(NU):
                    spread(i, par, u)
                    misc(u, i, par, post, pre)

            pe.wait_ge(s_prep, 1)
            embed(0)
            turn1(0)
            in_x(0, False)
            in_z(0, False)
            delta_bc(0, 0, 0)
            delta_bc(0, 0, 1)
            over_chunks(pe, lambda: body(0, 0, post=False), body, lambda: body(n_chunks - 1, 1, pre=False))
            for slot in range(NU):
                misc(slot, n_chunks, 0, True, False)

        @block.scalar
        def _(act):
            f = nc.scalar.activation

            def scale_x(c, half):
                cols_ = slice(half * XH, (half + 1) * XH)
                act.wait_ge(s_x_in, (c + 1) * 16)
                f(xs[:, cols_], xs[:, cols_], ACT.Identity, bias=round_col[:], scale=inv_alpha[:, 0:1]).then_inc(s_x_scaled, 1)

            def copy_turned(c, i):
                act.wait_ge([s_tr1, s_tr2][i], c + 1)
                f(xt[i][:], F[0], ACT.Copy).then_inc([s_xt1a, s_xt2a][i], 1)

            def x_evac(c):
                act.wait_ge(s_px_done, c + 1)
                wait(act, s_cv2_ready, c * 2)
                for part, (dst, src) in enumerate(((A, F[2]), (B, F[3][:, 0:HALF]))):
                    last = f(xin[:, dst], src, ACT.Identity, bias=col(cols, "in_b_x", part))
                last.then_inc(s_xin_ready, 1)
                wait(act, s_xc_ready, c)
                for part, (dst, src) in enumerate(((A, F[2]), (B, F[3][:, 0:HALF]))):
                    last = f(cv[:, dst], src, ACT.Identity, bias=conv_bias[:, part:part + 1],
                             scale=col(col_half, "conv_w1", part))
                last.then_inc(s_cv0_ready, 1)

            def z_evac(c):
                act.wait_ge(s_pz_done, c + 1)
                wait(act, s_zs_ready, c)
                srcs = ((A, F[0]), (B, F[1][:, 0:HALF]))
                for part, (dst, src) in enumerate(srcs):
                    last = f(zh[:, dst], src, ACT.Identity, bias=col(col_half, "in_b_z", part), scale=0.5)
                last.then_inc(s_zh_ready, 1)
                for part, (dst, src) in enumerate(srcs):
                    last = f(zt[:, dst], src, ACT.Tanh, bias=col(col_half, "in_b_z", part), scale=0.5)
                last.then_inc(s_zt_ready, 1)

            def conv_tanh(c):
                act.wait_ge(s_cv2_ready, (c + 1) * 2)
                f(cvt[:], cv[:], ACT.Tanh).then_inc(s_cvt_ready, 1)

            def delta_evac(c):
                act.wait_ge(s_pd_done, c + 1)
                wait(act, s_dt_ready, c)
                for part, (dst, src) in enumerate(((A, F[0]), (B, F[1][:, 0:HALF]))):
                    last = f(sp_ln[:, dst], src, ACT.Identity, bias=col(cols, "delta_b", part))
                last.then_inc(s_pd_read, 1)

            def softplus(c, step):
                if step == 0:
                    act.wait_ge(s_pd_read, c + 1)
                    f(sp_relu[:], sp_ln[:], ACT.Relu).then_inc(s_relu_ready, 1)
                if step == 1:
                    act.wait_ge(s_relu_ready, c + 1)
                    f(sp_ln[:], sp_ln[:], ACT.Abs).then_inc(s_abs_ready, 1)
                if step == 2:
                    act.wait_ge(s_abs_ready, c + 1)
                    f(sp_ln[:], sp_ln[:], ACT.Exp, scale=-1.0).then_inc(s_spe_ready, 1)
                if step == 3:
                    act.wait_ge(s_spe_ready, c + 1)
                    f(sp_ln[:], sp_ln[:], ACT.Ln, bias=1.0).then_inc(s_spl_ready, 1)

            def bc_high(c, par):
                act.wait_ge(s_pbc_done, c + 1)
                wait(act, s_c_spread, (c - 1) * NU)
                f(bc[par][:, :], F[2][0:96, :], ACT.Copy).then_inc(s_bc_hi, 1)

            def decays(c, par, u):
                kind, n = UNITS[u]
                if u == 0:
                    act.wait_ge(s_dt_ready, c + 1)
                wait(act, s_h_ready, c * NU + u - A_RING + 1)
                dst = images(decay[u % A_RING][:])
                src = images(dt[par][:])
                if kind == "A":
                    f(dst[:, :, 1:L], src[:, 0:8, 1:L], ACT.Exp, scale=a_neg[:, n:n + 1]).then_inc(s_decay_ready, 1)
                else:
                    for j in range(2):
                        last = f(dst[:, 4 * j:4 * j + 4, 1:L], src[:, 8:12, 1:L], ACT.Exp,
                                 scale=a_neg[:, N + n + j:N + n + j + 1])
                    last.then_inc(s_decay_ready, 1)

            def copy_c(c, u):
                act.wait_ge(s_c_spread, c * NU + u + 1)
                wait(act, s_hc_ready, c * NU + u - C_RING + 1)
                f(cs[u % C_RING][:], pc[:], ACT.Copy).then_inc(s_c_copied, 1)

            def gate_tanh(c):
                act.wait_ge(s_pg_done, c + 1)
                f(gt[:], pw[:, 0:TT * E], ACT.Tanh, scale=0.5).then_inc(s_gt_ready, 1)

            def cw_high(c):
                act.wait_ge(s_cwt_done, c + 1)
                f(cws[:, :], pw[0:96, :], ACT.Copy).then_inc(s_cw_hi, 1)

            def copy_cw(c, e):
                act.wait_ge(s_cw_spread, c * E + e + 1)
                if e >= 2:
                    act.wait_ge(s_eh_ready, c * E + e - 1)
                f(cwr[e % 2][:], pw[:], ACT.Copy).then_inc(s_cw_copied, 1)

            def expert_tanh(c, k):
                act.wait_ge(s_e1_done, c * EX + k + 1)
                if k:
                    act.wait_ge(s_eq_ready, c * EX + k)
                f(et[:], F[0], ACT.Tanh, scale=0.5).then_inc(s_et_ready, 1)

            def misc(slot, i, par, post, pre):
                if pre:
                    c = i + 1
                    if slot == 5:
                        copy_turned(c, 0)
                    if slot == 8:
                        x_evac(c)
                    if slot == 9:
                        z_evac(c)
                    if slot == 10:
                        conv_tanh(c)
                    if slot == 13:
                        delta_evac(c)
                        bc_high(c, 1 - par)
                    if slot in (17, 18):
                        scale_x(c + 1, slot - 17)
                    if slot in range(18, 22):
                        softplus(c, slot - 18)
                if post:
                    c = i - 1
                    if slot == 7:
                        copy_turned(c, 1)
                    if slot == 9:
                        gate_tanh(c)
                    if slot == 13:
                        cw_high(c)
                    for k in range(EX):
                        if slot == UP[k]:
                            expert_tanh(c, k)
                            if k:
                                copy_cw(c, k - 1)

            def body(i, par, post=True, pre=True):
                for u in range(NU):
                    if u + 1 < NU:
                        decays(i, par, u + 1)
                    elif pre:
                        decays(i + 1, 1 - par, 0)
                    copy_c(i, u)
                    misc(u, i, par, post, pre)

            act.wait_ge(s_w_in, W_ALL)
            f(a_neg[:], a_log[:], ACT.Exp).then_inc(s_avec_exp, 1)
            act.wait_ge(s_cols_ready, 1)
            f(tok_w[:], tok_w[:], ACT.Identity, bias=round_col[:], scale=inv_alpha[:, 1:2]).then_inc(s_tokw_scaled, 1)
            act.wait_ge(s_prep, 1)
            scale_x(0, 0)
            scale_x(0, 1)
            copy_turned(0, 0)
            x_evac(0)
            z_evac(0)
            conv_tanh(0)
            scale_x(1, 0)
            scale_x(1, 1)
            delta_evac(0)
            bc_high(0, 0)
            for step in range(4):
                softplus(0, step)
            decays(0, 0, 0)
            over_chunks(act, lambda: body(0, 0, post=False), body, lambda: body(n_chunks - 1, 1, pre=False))
            for slot in range(NU):
                misc(slot, n_chunks, 0, True, False)

        @block.vector
        def _(dve):
            v = nc.vector

            def quantise(c, half):
                cols_ = slice(half * XH, (half + 1) * XH)
                dve.wait_ge(s_x_scaled, 2 * c + half + 1)
                wait(dve, s_conv_done, c)
                v.tensor_scalar(xq[:, cols_], xs[:, cols_], ROUND, 127.0, ALU.subtract, ALU.min).then_inc(s_xq_top, 1)
                dve.wait_ge(s_xq_top, 2 * c + half + 1)
                v.tensor_scalar(xq[:, cols_], xq[:, cols_], -128.0, None, ALU.max).then_inc(s_xq_ready, 1)

            def embed_out(c, par):
                dve.wait_ge(s_conv_done, c + 1)
                wait(dve, s_h0b_ready, c - 1)
                for i in range(2):
                    dst = h0[par][:, 2 * i:2 * i + 2, :].rearrange("p t d -> p (t d)")
                    last = v.scalar_tensor_tensor(dst, F[2 + i][:, 0:2 * D], alpha_prod[:, 0:1], tok_b[:],
                                                  ALU.mult, ALU.add)
                last.then_inc(s_h0_ready, 1)

            def norm_stats(c, i, src, src_sem):
                st_sem, mv_sem, ve_sem = [(s_st1, s_mv1, s_ve1), (s_st2, s_mv2, s_ve2)][i]
                dve.wait_ge(src_sem, c + 1)
                for tt in range(TT):
                    last = v.bn_stats(stats[i][:, tt, :], src[:, tt, :])
                last.then_inc(st_sem, 1)
                dve.wait_ge(st_sem, c + 1)
                dve.sem_inc(s_stats_seen, 1)
                for tt in range(TT):
                    last = v.bn_aggr(mv[i][:, tt, :], stats[i][:, tt, :])
                last.then_inc(mv_sem, 1)
                dve.wait_ge(mv_sem, c + 1)
                v.tensor_scalar(vare[i][:], mv[i][:, :, 1], LN_EPS, None, ALU.add).then_inc(ve_sem, 1)

            def norm_apply(c, i, src):
                dve.wait_ge([s_mv1, s_mv2][i], c + 1)
                dve.wait_ge([s_rs1, s_rs2][i], c + 1)
                for tt in range(TT):
                    last = v.tensor_scalar(xn[i][:, tt, :], src[:, tt, :], mv[i][:, tt, 0:1],
                                           rstd[i][:, tt:tt + 1], ALU.subtract, ALU.mult)
                last.then_inc([s_xn1, s_xn2][i], 1)

            def copy_turned(c, i):
                dve.wait_ge([s_tr1, s_tr2][i], c + 1)
                v.tensor_copy(xtr[i][:], F[1][0:DR, :]).then_inc([s_xt1b, s_xt2b][i], 1)

            def conv(c):
                dve.wait_ge(s_xin_ready, c + 1)
                dve.wait_ge(s_cv0_ready, c + 1)
                for name, dst_l, src_l, done in (("conv_w0", slice(1, L), slice(0, L - 1), s_cv1_ready),
                                                 ("conv_w2", slice(0, L - 1), slice(1, L), s_cv2_ready)):
                    for part, cols_ in enumerate((A, B)):
                        o = images(cv[:, cols_])[:, :, dst_l]
                        ins = v.scalar_tensor_tensor(o, images(xin[:, cols_])[:, :, src_l],
                                                     col(col_half, name, part), o, ALU.mult, ALU.add)
                        ins.then_inc(done, 1)
                    if done is s_cv1_ready:
                        dve.wait_ge(s_cv1_ready, (c + 1) * 2)

            def conv_gate(c, par):
                dve.wait_ge(s_cvt_ready, c + 1)
                wait(dve, s_ys_ready, c - 1)
                v.scalar_tensor_tensor(xc[par][:], cvt[:], 1.0, cv[:], ALU.add, ALU.mult).then_inc(s_xc_ready, 1)

            def z_gate(c, par):
                dve.wait_ge(s_zt_ready, c + 1)
                dve.wait_ge(s_zh_ready, c + 1)
                wait(dve, s_yg_ready, c - 1)
                v.scalar_tensor_tensor(zs[par][:], zt[:], 1.0, zh[:], ALU.add, ALU.mult).then_inc(s_zs_ready, 1)

            def split(c, src, hi, r, m, sems, step):
                hi_sem, r_sem, m_sem, mid_sem, done = sems
                if step == 0:
                    dve.wait_ge(hi_sem, c + 1)
                    v.tensor_tensor(r[:], src, hi[:], ALU.subtract).then_inc(r_sem, 1)
                    return
                dve.wait_ge(r_sem, c + 1)
                v.tensor_copy(m[:], r[:]).then_inc(m_sem, 1)
                dve.wait_ge(m_sem, c + 1)
                v.tensor_copy(hi[32:64, :], m[32:64, :]).then_inc(mid_sem, 1)
                dve.wait_ge(mid_sem, c + 1)
                v.tensor_tensor(hi[64:96, :], r[64:96, :], m[64:96, :], ALU.subtract).then_inc(done, 1)

            def split_bc(c, par, step):
                split(c, F[2][0:96, :], bc[par], split_r, split_m, (s_bc_hi, s_bc_r, s_bc_m, s_bc_mid, s_bc_ready), step)

            def split_cw(c, step):
                split(c, pw[0:96, :], cws, csplit_r, csplit_m, (s_cw_hi, s_cw_r, s_cw_m, s_cw_mid, s_cw_parts), step)

            def step_sizes(c, par):
                dve.wait_ge(s_relu_ready, c + 1)
                dve.wait_ge(s_spl_ready, c + 1)
                wait(dve, s_decay_ready, (c - 1) * NU)
                v.tensor_tensor(dt[par][:], sp_relu[:], sp_ln[:], ALU.add).then_inc(s_dt_ready, 1)
                dve.wait_ge(s_dt_ready, c + 1)
                wait(dve, s_b_times_u, (c - 1) * NU)
                v.tensor_tensor(ut[par][:], dt[par][:], xc[par][:], ALU.mult).then_inc(s_ut_ready, 1)

            def scan(c, par, u):
                kind, n = UNITS[u]
                b = pb[u % 2]
                if u == 0:
                    dve.wait_ge(s_ut_ready, c + 1)
                dve.wait_ge(s_b_spread, c * NU + u + 1)
                if kind == "A":
                    v.tensor_tensor(b[:], b[:], ut[par][:, A], ALU.mult).then_inc(s_b_times_u, 1)
                else:
                    two = b[:].rearrange("p (j m) -> p j m", j=2)
                    v.tensor_tensor(two, two, ut[par][:, B].unsqueeze(1).broadcast_to([P, 2, HALF]),
                                    ALU.mult).then_inc(s_b_times_u, 1)
                dve.wait_ge(s_decay_ready, c * NU + u + 1)
                wait(dve, s_hc_ready, c * NU + u - H_RING + 1)
                dve.wait_ge(s_b_times_u, c * NU + u + 1)
                v.tensor_tensor_scan(hs[u % H_RING][:], decay[u % A_RING][:], b[:], 0.0,
                                     ALU.mult, ALU.add).then_inc(s_h_ready, 1)

            def mixer_out(c, par):
                dve.wait_ge(s_y_added, added(c, NU - 1))
                v.tensor_tensor(ys[:, B], ya[par][:, CH:CH + HALF], ya[par][:, CH + HALF:], ALU.add)\
                    .then_inc(s_yb_ready, 1)
                v.scalar_tensor_tensor(ys[:, A], xc[par][:, A], col(cols, "D_param", 0), ya[par][:, A],
                                       ALU.mult, ALU.add)
                dve.wait_ge(s_yb_ready, c + 1)
                v.scalar_tensor_tensor(ys[:, B], xc[par][:, B], col(cols, "D_param", 1), ys[:, B],
                                       ALU.mult, ALU.add).then_inc(s_ys_ready, 1)
                dve.wait_ge(s_ys_ready, c + 1)
                v.tensor_tensor(yg[:], ys[:], zs[par][:], ALU.mult).then_inc(s_yg_ready, 1)

            def residual(c):
                dve.wait_ge(s_po_done, c + 1)
                dve.wait_ge(s_h0b_ready, c + 1)
                dve.wait_ge(s_out_stored, c * 16 + 1)
                for i in range(2):
                    last = v.tensor_tensor(h1[:, 2 * i:2 * i + 2, :], bank_pair(i), h0b[:, 2 * i:2 * i + 2, :], ALU.add)
                last.then_inc(s_h1_ready, 1)

            def beats(c, gt_, ge_, values, n, before, sems, keep=None):
                gt_sem, ge_sem, m_sem = sems
                other = values.unsqueeze(2).broadcast_to([P, TT, n, n])
                own = values.unsqueeze(3).broadcast_to([P, TT, n, n])
                lower = before[:].rearrange("p (a b) -> p a b", a=n).unsqueeze(1).broadcast_to([P, TT, n, n])
                v.tensor_tensor(gt_[:], other, own, ALU.is_gt).then_inc(gt_sem, 1)
                v.tensor_tensor(ge_[:], other, own, ALU.is_ge).then_inc(ge_sem, 1)
                dve.wait_ge(ge_sem, 2 * c + 1)
                v.tensor_tensor(ge_[:], ge_[:], lower, ALU.mult).then_inc(ge_sem, 1)
                dve.wait_ge(ge_sem, 2 * c + 2)
                dve.wait_ge(gt_sem, c + 1)
                v.tensor_tensor(gt_[:], gt_[:], ge_[:], ALU.max).then_inc(m_sem, 1)
                dve.wait_ge(m_sem, c + 1)

            def route_groups(c):
                dve.wait_ge(s_gt_ready, c + 1)
                v.tensor_scalar(score[:].rearrange("p t e -> p (t e)"), gt[:], 0.5, 0.5, ALU.mult,
                                ALU.add).then_inc(s_score_ready, 1)
                dve.wait_ge(s_score_ready, c + 1)
                v.tensor_tensor(biased[:], score[:], gate_b[:].rearrange("p (t e) -> p t e", e=E),
                                ALU.add).then_inc(s_biased_ready, 1)
                dve.wait_ge(s_biased_ready, c + 1)
                pairs = biased[:].rearrange("p t (g j) -> p t g j", j=2)
                v.tensor_tensor(gsum[:], pairs[:, :, :, 0], pairs[:, :, :, 1], ALU.add).then_inc(s_gsum_ready, 1)
                dve.wait_ge(s_gsum_ready, c + 1)
                beats(c, g_gt, g_ge, gsum[:], 4, before4, (s_ggt_ready, s_gge_ready, s_gm_ready))
                v.tensor_reduce(g_rank[:], g_gt[:], AX.X, ALU.add).then_inc(s_grank_ready, 1)
                dve.wait_ge(s_grank_ready, c + 1)
                v.tensor_scalar(g_sel[:], g_rank[:], 2.0, None, ALU.is_lt).then_inc(s_gsel_ready, 1)

            def route_experts(c):
                dve.wait_ge(s_gsel_ready, c + 1)
                beats(c, e_gt, e_ge, biased[:], 8, before8, (s_egt_ready, s_ege_ready, s_em_ready))
                sel_b = g_sel[:].unsqueeze(3).broadcast_to([P, TT, 4, 2])
                v.tensor_copy(e_sel[:].rearrange("p t (g j) -> p t g j", j=2), sel_b).then_inc(s_esel_ready, 1)
                dve.wait_ge(s_esel_ready, c + 1)
                v.tensor_tensor(e_gt[:], e_gt[:], e_sel[:].unsqueeze(2).broadcast_to([P, TT, 8, 8]),
                                ALU.mult).then_inc(s_ems_ready, 1)
                dve.wait_ge(s_ems_ready, c + 1)
                v.tensor_reduce(e_rank[:], e_gt[:], AX.X, ALU.add).then_inc(s_erank_ready, 1)
                dve.wait_ge(s_erank_ready, c + 1)
                v.scalar_tensor_tensor(e_sel[:], e_rank[:], 2.0, e_sel[:], ALU.is_lt, ALU.mult)\
                    .then_inc(s_esel2_ready, 1)
                dve.wait_ge(s_esel2_ready, c + 1)
                v.tensor_tensor(e_w[:], e_sel[:], score[:], ALU.mult).then_inc(s_ew_ready, 1)
                dve.wait_ge(s_ew_ready, c + 1)
                v.tensor_reduce(wsum[:], e_w[:], AX.X, ALU.add).then_inc(s_wsum_ready, 1)
                dve.wait_ge(s_wsum_ready, c + 1)
                v.tensor_scalar(wsum[:], wsum[:], 1e-6, None, ALU.add).then_inc(s_weps_ready, 1)
                dve.wait_ge(s_weps_ready, c + 1)
                v.reciprocal(winv[:], wsum[:]).then_inc(s_winv_ready, 1)
                dve.wait_ge(s_winv_ready, c + 1)
                for copy in range(3):
                    last = v.tensor_tensor(cw3[:, :, copy, 0:E], e_w[:], winv[:].unsqueeze(2).broadcast_to([P, TT, E]),
                                           ALU.mult)
                last.then_inc(s_cw_ready, 1)

            def expert_mul(c, k):
                dve.wait_ge(s_et_ready, c * EX + k + 1)
                if k:
                    dve.wait_ge(s_eg_ready, c * EX + k)
                v.scalar_tensor_tensor(eq[:], et[:], 1.0, F[0], ALU.add, ALU.mult).then_inc(s_eq_ready, 1)
                dve.wait_ge(s_e3_done, c * EX + k + 1)
                dve.wait_ge(s_eq_ready, c * EX + k + 1)
                if k >= 3:
                    dve.wait_ge(s_eh_ready, c * E + k - 2)
                v.tensor_tensor(eg[k % 2][:] if k else eh[0][:], eq[:], F[1], ALU.mult).then_inc(s_eg_ready, 1)

            def finish(c):
                dve.wait_ge(s_e2_done, (c + 1) * EX)
                for i in range(2):
                    last = v.tensor_tensor(h1[:, 2 * i:2 * i + 2, :], bank_pair(i), h1[:, 2 * i:2 * i + 2, :], ALU.add)
                last.then_inc(s_out_ready, 1)

            def misc(slot, i, par, post, pre):
                if pre:
                    c = i + 1
                    if slot == 2:
                        embed_out(c, 1 - par)
                        norm_stats(c, 0, h0[1 - par], s_h0_ready)
                    if slot == 3:
                        norm_apply(c, 0, h0[1 - par])
                    if slot == 5:
                        copy_turned(c, 0)
                    if slot == 9:
                        conv(c)
                    if slot == 10:
                        conv_gate(c, 1 - par)
                        z_gate(c, 1 - par)
                    if slot in (13, 15):
                        split_bc(c, 1 - par, slot > 13)
                    if slot in (18, 19):
                        quantise(c + 1, slot - 18)
                    if slot == 22:
                        step_sizes(c, 1 - par)
                if post:
                    c = i - 1
                    if slot == 1:
                        mixer_out(c, 1 - par)
                    if slot == 4:
                        residual(c)
                        norm_stats(c, 1, h1, s_h1_ready)
                    if slot == 5:
                        norm_apply(c, 1, h1)
                    if slot == 7:
                        copy_turned(c, 1)
                    if slot == 11:
                        route_groups(c)
                    if slot == 12:
                        route_experts(c)
                    if slot in (13, 14):
                        split_cw(c, slot - 13)
                    if slot == UP[0]:
                        expert_mul(c, 0)
                    for k in range(1, EX):
                        if slot == UP[k]:
                            expert_mul(c, k)
                    if slot == 23:
                        finish(c)

            def body(i, par, post=True, pre=True):
                for u in range(NU):
                    scan(i, par, u)
                    misc(u, i, par, post, pre)

            v.memset(round_col[:], ROUND)
            v.memset(neg_half[:], -0.5).then_inc(s_out_ready, 1)
            v.memset(cw3[:].rearrange("p a b c -> p (a b c)"), 0.0)
            for i in range(A_RING):
                v.memset(decay[i][:], 0.0)
            dve.wait_ge(s_w_in, W_ALL)
            v.reciprocal(inv_alpha[:], alphas[:])
            v.tensor_tensor(alpha_prod[:], alphas[:, 0:1], alphas[:, 1:2], ALU.mult)
            v.tensor_scalar(col_half[:], cols[:], 0.5, None, ALU.mult)
            v.tensor_scalar(w2[:], w2[:], 0.5, None, ALU.mult).then_inc(s_cols_ready, 1)
            dve.wait_ge(s_cols_ready, 1)
            ib, cw1, cb = (2 * COLS.index(n) for n in ("in_b_x", "conv_w1", "conv_b"))
            v.tensor_tensor(conv_bias[:], cols[:, ib:ib + 2], col_half[:, cw1:cw1 + 2], ALU.mult).then_inc(s_consts, 1)
            dve.wait_ge(s_consts, 1)
            v.tensor_tensor(conv_bias[:], conv_bias[:], col_half[:, cb:cb + 2], ALU.add).then_inc(s_consts, 1)
            dve.wait_ge(s_avec_exp, 1)
            v.tensor_scalar(a_neg[:], a_neg[:], -1.0, None, ALU.mult).then_inc(s_avec_ready, 1)
            dve.wait_ge(s_tokw_scaled, 1)
            v.tensor_scalar(tok_w[:], tok_w[:], ROUND, 127.0, ALU.subtract, ALU.min).then_inc(s_tokw_clamped, 1)
            dve.wait_ge(s_tokw_clamped, 1)
            dve.wait_ge(s_avec_ready, 1)
            dve.wait_ge(s_consts, 2)
            v.tensor_scalar(tok_wq[:], tok_w[:], -128.0, None, ALU.max).then_inc(s_prep, 1)

            quantise(0, 0)
            quantise(0, 1)
            embed_out(0, 0)
            norm_stats(0, 0, h0[0], s_h0_ready)
            norm_apply(0, 0, h0[0])
            copy_turned(0, 0)
            conv(0)
            conv_gate(0, 0)
            z_gate(0, 0)
            quantise(1, 0)
            quantise(1, 1)
            split_bc(0, 0, 0)
            split_bc(0, 0, 1)
            step_sizes(0, 0)
            over_chunks(dve, lambda: body(0, 0, post=False), body, lambda: body(n_chunks - 1, 1, pre=False))
            for slot in range(NU):
                misc(slot, n_chunks, 0, True, False)

        @block.gpsimd
        def _(pool):
            g = nc.gpsimd

            def inv_std(c, i):
                ve_sem, rs_sem = [(s_ve1, s_rs1), (s_ve2, s_rs2)][i]
                pool.wait_ge(ve_sem, c + 1)
                g.tensor_tensor(rstd[i][:], vare[i][:], neg_half[:], ALU.pow).then_inc(rs_sem, 1)

            def with_out_b(c, par):
                pool.wait_ge(s_h0_ready, c + 1)
                flat = "p t d -> p (t d)"
                g.tensor_tensor(h0b[:].rearrange(flat), h0[par][:].rearrange(flat), out_b[:], ALU.add)\
                    .then_inc(s_h0b_ready, 1)

            def times_c(c, par, u):
                kind = UNITS[u][0]
                pool.wait_ge(s_h_ready, c * NU + u + 1)
                pool.wait_ge(s_c_copied, c * NU + u + 1)
                if u == 0:
                    wait(pool, s_ys_ready, c - 1)
                wait(pool, s_y_added, added(c, u - Y_RING))
                dst = state_sum(par, kind) if u in (0, 2) else hc[u % Y_RING][:]
                g.tensor_tensor(dst, hs[u % H_RING][:], cs[u % C_RING][:], ALU.mult).then_inc(s_hc_ready, 1)

            def state_sum(par, kind):
                return ya[par][:, 0:CH] if kind == "A" else ya[par][:, CH:2 * CH]

            def add_y(c, par, u):
                if u in (0, 2):
                    return
                pool.wait_ge(s_hc_ready, c * NU + u + 1)
                if u > 1:
                    pool.wait_ge(s_y_added, added(c, u - 1))
                dst = state_sum(par, UNITS[u][0])
                g.tensor_tensor(dst, dst, hc[u % Y_RING][:], ALU.add).then_inc(s_y_added, 1)

            def expert_weight(c, k):
                pool.wait_ge(s_eg_ready, c * EX + k + 1)
                pool.wait_ge(s_cw_copied, c * E + k)
                if k >= 2:
                    pool.wait_ge(s_e2_done, c * EX + k - 1)
                g.tensor_tensor(eh[k % 2][:], eg[k % 2][:], cwr[(k - 1) % 2][:], ALU.mult).then_inc(s_eh_ready, 1)

            def misc(slot, i, par, post, pre):
                if pre and slot == 2:
                    inv_std(i + 1, 0)
                if post:
                    c = i - 1
                    if slot == 1:
                        with_out_b(c, 1 - par)
                    if slot == 4:
                        inv_std(c, 1)
                    for k in range(1, EX):
                        if slot == UP[k]:
                            expert_weight(c, k)

            def body(i, par, post=True, pre=True):
                for u in range(NU):
                    times_c(i, par, u)
                    if u >= 1:
                        add_y(i, par, u - 1)
                    elif post:
                        add_y(i - 1, 1 - par, NU - 1)
                    misc(u, i, par, post, pre)

            pool.wait_ge(s_prep, 1)
            inv_std(0, 0)
            over_chunks(pool, lambda: body(0, 0, post=False), body, lambda: body(n_chunks - 1, 1, pre=False))
            add_y(n_chunks - 1, 1, NU - 1)
            for slot in range(NU):
                misc(slot, n_chunks, 0, True, False)


def kernel(**inputs):
    import numpy as np
    import ml_dtypes
    import concourse.bacc as bacc
    from concourse.bass_utils import run_bass_kernel_spmd

    a = {k: np.asarray(v) for k, v in inputs.items()}
    f32 = np.float32

    def twice(m):
        return np.stack([m[:P], np.concatenate([m[P:], m[P:]])], axis=1)

    def on_all(v):
        return np.broadcast_to(np.ravel(v), (P, np.size(v)))

    n_img = a["x"].shape[0]
    n_chunks = n_img * L // CH
    x = a["x"].reshape(n_chunks, CH // L, 3, 8, 16, 8, 16).transpose(0, 2, 4, 6, 1, 3, 5)
    x = x.reshape(n_chunks, KT, P, CH).transpose(0, 2, 1, 3).reshape(n_chunks, P, KT * CH)
    tok_w = a["L0_tok_W"].reshape(D, KT, P).transpose(2, 1, 0).reshape(P, KT * D)
    in_b, conv_w = a["L0_attn_in_b"], a["L0_attn_conv_w"]
    vectors = [in_b[:D], in_b[D:], conv_w[:, 0, 0], conv_w[:, 0, 1], conv_w[:, 0, 2],
               a["L0_attn_conv_b"], a["L0_attn_delta_b"], a["L0_attn_D_param"]]
    bc_w = np.concatenate([a["L0_attn_B_proj_w"], a["L0_attn_C_proj_w"]] * 3).T
    w1 = np.concatenate([a["L0_ffn_w1"], a["L0_ffn_sw1"][None]])
    w3 = np.concatenate([a["L0_ffn_w3"], a["L0_ffn_sw3"][None]])
    w2 = np.concatenate([a["L0_ffn_w2"], a["L0_ffn_sw2"][None]])
    sel = np.zeros((96, 2 * N, P), ml_dtypes.bfloat16)
    for part in range(3):
        for r in range(2 * N):
            sel[32 * part + r, r, :] = 1
    laid = {
        "x": x, "ident": np.eye(P, dtype=f32), "sel": sel,
        "cols": np.stack([twice(v) for v in vectors], axis=1).reshape(P, NCOL),
        "alphas": on_all(np.stack([a["L0_tok_alpha_a"], a["L0_tok_alpha_w"]])),
        "a_log": twice(a["L0_attn_A_log"]).reshape(P, 2 * N),
        "tok_w": tok_w, "tok_b": on_all(np.stack([a["L0_tok_b"]] * 2)),
        "out_b": on_all(np.stack([a["L0_attn_out_b"]] * TT)),
        "in_w": twice(a["L0_attn_in_w"].T), "delta_w": twice(a["L0_attn_delta_w"].T),
        "bc_w": twice(bc_w), "out_w": twice(a["L0_attn_out_w"].T),
        "gate_w": twice(a["L0_ffn_gate_weight"].T), "gate_b": on_all(np.stack([a["L0_ffn_gate_bias"]] * TT)),
        "before4": on_all(np.tril(np.ones((4, 4), f32), -1)), "before8": on_all(np.tril(np.ones((8, 8), f32), -1)),
        "w1": twice(w1.transpose(2, 0, 1)), "w3": twice(w3.transpose(2, 0, 1)), "w2": w2.transpose(2, 0, 1),
    }
    nc = bacc.Bacc("TRN2", target_bir_lowering=False, num_devices=1)
    arrays, aps = {}, {}
    for name, value in laid.items():
        value = np.ascontiguousarray(value)
        arrays[f"in_{name}_dram"] = value
        aps[name] = nc.dram_tensor(f"in_{name}_dram", value.shape, mybir.dt.from_np(value.dtype),
                                   kind="ExternalInput").ap()
    out = nc.dram_tensor("out_0_dram", (n_img, L, D), F32, kind="ExternalOutput").ap()
    out_v = out.rearrange("(c m) l d -> c (m l) d", c=n_chunks).rearrange("c (t p) d -> c p t d", p=P)
    build(nc, aps, out_v)
    got = run_bass_kernel_spmd(nc, [arrays], core_ids=[0])
    return got.results[0]["out_0_dram"]
```

```python
from contextlib import ExitStack

import concourse.bass as bass
from concourse import mybir

F32 = mybir.dt.float32
BF16 = mybir.dt.bfloat16
F16 = mybir.dt.float16
I32 = mybir.dt.int32
ALU = mybir.AluOpType
ACT = mybir.ActivationFunctionType
AX = mybir.AxisListType

P = 128
D = 192
DR = D - P
L = 64
CH = 512
HALF = CH // 2
PK = CH + HALF
TT = CH // P
KT = 768 // P
XH = KT * CH // 2
N = 16
E = 8
EX = E + 1
ROUND = 1.5 * 2 ** 23
LN_EPS = 1e-5
W_TOP = 2.0 ** 13
EXPONENT = 0x7F800000

UNITS = [u for m in range(0, N, 2) for u in (("A", m), ("A", m + 1), ("B", m))]
NU = len(UNITS)
A_RING, H_RING, C_RING, Y_RING = 3, 3, 3, 2

UP = list(range(12, 12 + EX))
DOWN = [u + 1 for u in UP]
PE_AT = dict(out_proj=2, turn1=3, in_x=4, in_z=5, turn2=7, gate=8, delta0=9, delta1=10, turn_cw=11,
             embed=23)
ACT_AT = dict(norm_apply1=2, copy1=3, x_evac=5, z_evac=6, conv_tanh=6, copy2=7, gate_tanh=8,
              delta_evac=11, bc_high=13, cw_high=11, scale_x0=16, scale_x1=17, relu=18, abs=19,
              exp=21, ln=21, y_init=14, norm_apply2=5)
DVE_AT = dict(embed_out=1, mixer_out=1, stats1=1, residual=3, stats2=4, conv=6, conv_gate=7,
              z_gate=7, copy2=7, x_low=8, route_groups=10, route_experts=10, bc_rest=13,
              bc_parts=16, cw_rest=11, cw_parts=13, quantise0=18, quantise1=20, step_sizes=22,
              finish=22)
POOL_AT = dict(inv_std1=1, inv_std2=4, with_out_b=8)

COLS = ["in_b_x", "in_b_z", "conv_w0", "conv_w1", "conv_w2", "conv_b", "delta_b", "D_param"]
NCOL = 2 * len(COLS)


def build(nc, t, out):
    n_chunks = t["x"].shape[0]
    ctx = ExitStack()
    with ctx:
        def sb(name, shape, dt=F32):
            return ctx.enter_context(nc.sbuf_tensor(name, shape, dt))

        ident = sb("ident", [P, P])
        sel = sb("sel", [96, 2 * N, P], BF16)
        cols = sb("cols", [P, NCOL])
        col_half = sb("col_half", [P, NCOL])
        conv_bias = sb("conv_bias", [P, 2])
        alphas = sb("alphas", [P, 2])
        inv_alpha = sb("inv_alpha", [P, 2])
        alpha_prod = sb("alpha_prod", [P, 1])
        round_col = sb("round_col", [P, 1])
        a_log = sb("a_log", [P, 2 * N])
        a_neg = sb("a_neg", [P, 2 * N])
        tok_w = sb("tok_w", [P, KT * D])
        tok_wq = sb("tok_wq", [P, KT * D], BF16)
        tok_b = sb("tok_b", [P, 2 * D])
        out_b = sb("out_b", [P, TT * D])
        in_w = sb("in_w", [P, 2, 2 * D])
        delta_w = sb("delta_w", [P, 2, D])
        bc_w = sb("bc_w", [P, 2, 96])
        out_w = sb("out_w", [P, 2, D])
        gate_w = sb("gate_w", [P, 2, E])
        gate_b = sb("gate_b", [P, TT * E])
        before4 = sb("before4", [P, 16])
        before8 = sb("before8", [P, 64])
        w13_hi = [sb(f"w{i}_hi", [P, 2, EX, P], F16) for i in (1, 3)]
        w13_lo = [sb(f"w{i}_lo", [P, 2, EX, P], F16) for i in (1, 3)]
        w_peak = sb("w_peak", [P, 4])
        w_scale = sb("w_scale", [P, 1])
        w_unscale = sb("w_unscale", [P, 1])
        half_unscale = sb("half_unscale", [P, 1])
        w2 = sb("w2", [P, EX, D])
        neg_half = sb("neg_half", [P, TT])

        xs = sb("xs", [P, KT * CH])
        xq = sb("xq", [P, KT * CH], BF16)
        h0 = [sb(f"h0_{i}", [P, TT, D]) for i in range(2)]
        h0b = sb("h0b", [P, TT, D])
        stats = [sb(f"stats{i}", [P, TT, 6]) for i in range(2)]
        mv = [sb(f"mv{i}", [P, TT, 2]) for i in range(2)]
        vare = [sb(f"vare{i}", [P, TT]) for i in range(2)]
        neg_mean = [sb(f"neg_mean{i}", [P, TT]) for i in range(2)]
        shift = [sb(f"shift{i}", [P, TT]) for i in range(2)]
        rstd = [sb(f"rstd{i}", [P, TT]) for i in range(2)]
        xn = [sb(f"xn{i}", [P, TT, D]) for i in range(2)]
        xt1 = sb("xt1", [P, CH])
        xtr = [sb(f"xtr{i}", [DR, CH]) for i in range(2)]
        x_hi = sb("x_hi", [P, CH], F16)
        x_lo = sb("x_lo", [P, CH], F16)
        x_rest = sb("x_rest", [P, CH], F16)
        xin = sb("xin", [P, PK])
        cv = sb("cv", [P, PK])
        cvt = sb("cvt", [P, PK])
        zh = sb("zh", [P, PK])
        zt = sb("zt", [P, PK])
        sp_relu, sp_ln = zh, cvt
        xc = [sb(f"xc{i}", [P, PK]) for i in range(2)]
        zs = [sb(f"zs{i}", [P, PK]) for i in range(2)]
        dt = [sb(f"dt{i}", [P, PK]) for i in range(2)]
        ut = [sb(f"ut{i}", [P, PK]) for i in range(2)]
        bc = [sb(f"bc{i}", [96, CH], BF16) for i in range(2)]
        split_r = sb("split_r", [96, CH])
        split_m = sb("split_m", [96, CH], BF16)
        decay, hs, cs, hc = ([sb(f"{name}{i}", [P, CH])[:] for i in range(size)] for name, size in (
            ("decay", A_RING), ("hs", H_RING), ("cs", C_RING), ("hc", Y_RING)))
        work = sb("work", [P, 9, CH])
        et, eq, eg, eh0, eh1, xt2 = (work[:, i, :] for i in range(6))
        eh = (eh0, eh1)
        w13 = work[:].rearrange("p a b -> p (a b)")[:, 0:4 * EX * P]
        w13_f32 = [w13[:, i * 2 * EX * P:(i + 1) * 2 * EX * P].rearrange("p (k e m) -> p k e m", k=2, e=EX)
                   for i in range(2)]
        xt = (xt1[:], xt2)
        ya = [sb(f"ya{i}", [P, 2 * CH]) for i in range(2)]
        yb = sb("yb", [P, HALF])
        yg = sb("yg", [P, PK])
        h1 = sb("h1", [P, TT, D])
        gt = sb("gt", [P, TT * E])
        score = sb("score", [P, TT, E])
        biased = sb("biased", [P, TT, E])
        gsum = sb("gsum", [P, TT, 4])
        g_gt = sb("g_gt", [P, TT, 4, 4])
        g_ge = sb("g_ge", [P, TT, 4, 4])
        g_rank = sb("g_rank", [P, TT, 4])
        g_sel = sb("g_sel", [P, TT, 4])
        e_gt = sb("e_gt", [P, TT, 8, 8])
        e_ge = sb("e_ge", [P, TT, 8, 8])
        e_rank = sb("e_rank", [P, TT, E])
        e_sel = sb("e_sel", [P, TT, E])
        e_w = sb("e_w", [P, TT, E])
        wsum = sb("wsum", [P, TT])
        winv = sb("winv", [P, TT])
        cw3 = sb("cw3", [P, TT, 3, 32])
        cws = sb("cws", [96, CH], BF16)
        csplit_r = sb("csplit_r", [96, CH])
        csplit_m = sb("csplit_m", [96, CH], BF16)

        pb = [ctx.enter_context(nc.psum_tensor(f"pb{i}", [P, CH], F32)) for i in range(2)]
        pc = ctx.enter_context(nc.psum_tensor("pc", [P, CH], F32))
        pw = ctx.enter_context(nc.psum_tensor("pw", [P, CH], F32))
        pf = ctx.enter_context(nc.psum_tensor("pf", [P, 4, 512], F32))
        F = [pf[:, i, :] for i in range(4)]

        def sem(name):
            return ctx.enter_context(nc.semaphore(name))

        s_w_embed = sem("w_embed")
        s_w_mixer = sem("w_mixer")
        s_w_experts = sem("w_experts")
        s_w_post = sem("w_post")
        s_peak_in = sem("peak_in")
        s_peak_ready = sem("peak_ready")
        s_peak_diag = sem("peak_diag")
        s_peak_spread = sem("peak_spread")
        s_peak_all = sem("peak_all")
        s_scale_ready = sem("scale_ready")
        s_w2_ready = sem("w2_ready")
        s_w13_scaled = sem("w13_scaled")
        s_w13_hi = sem("w13_hi")
        s_w13_ready = sem("w13_ready")
        s_consts = sem("consts")
        s_tokw_scaled = sem("tokw_scaled")
        s_tokw_clamped = sem("tokw_clamped")
        s_avec_exp = sem("avec_exp")
        s_avec_ready = sem("avec_ready")
        s_cols_ready = sem("cols_ready")
        s_prep = sem("prep")
        s_mixer_prep = sem("mixer_prep")
        s_x_in = sem("x_in")
        s_x_scaled = sem("x_scaled")
        s_xq_top = sem("xq_top")
        s_xq_ready = sem("xq_ready")
        s_conv_done = sem("conv_done")
        s_h0_ready = sem("h0_ready")
        s_stats_seen = sem("stats_seen")
        s_st1 = sem("st1")
        s_mv1 = sem("mv1")
        s_ve1 = sem("ve1")
        s_nm1 = sem("nm1")
        s_nm2 = sem("nm2")
        s_pow1 = sem("pow1")
        s_pow2 = sem("pow2")
        s_rs1 = sem("rs1")
        s_xn1 = sem("xn1")
        s_tr1 = sem("tr1")
        s_xt1a = sem("xt1a")
        s_xt1b = sem("xt1b")
        s_px_done = sem("px_done")
        s_pz_done = sem("pz_done")
        s_xin_ready = sem("xin_ready")
        s_cv0_ready = sem("cv0_ready")
        s_cv1_ready = sem("cv1_ready")
        s_cv2_ready = sem("cv2_ready")
        s_cvt_ready = sem("cvt_ready")
        s_xc_ready = sem("xc_ready")
        s_zh_ready = sem("zh_ready")
        s_zt_ready = sem("zt_ready")
        s_zs_ready = sem("zs_ready")
        s_lower_rows = sem("lower_rows")
        s_pd_done = sem("pd_done")
        s_pbc_done = sem("pbc_done")
        s_pd_read = sem("pd_read")
        s_relu_ready = sem("relu_ready")
        s_abs_ready = sem("abs_ready")
        s_spe_ready = sem("spe_ready")
        s_spl_ready = sem("spl_ready")
        s_dt_ready = sem("dt_ready")
        s_ut_ready = sem("ut_ready")
        s_bc_hi = sem("bc_hi")
        s_bc_r = sem("bc_r")
        s_bc_m = sem("bc_m")
        s_bc_mid = sem("bc_mid")
        s_bc_ready = sem("bc_ready")
        s_decay_ready = sem("decay_ready")
        s_b_spread = sem("b_spread")
        s_c_spread = sem("c_spread")
        s_b_times_u = sem("b_times_u")
        s_h_ready = sem("h_ready")
        s_c_copied = sem("c_copied")
        s_hc_ready = sem("hc_ready")
        s_y_added = sem("y_added")
        s_yb_ready = sem("yb_ready")
        s_y_init = sem("y_init")
        s_yg_ready = sem("yg_ready")
        s_po_done = sem("po_done")
        s_h0b_ready = sem("h0b_ready")
        s_h1_ready = sem("h1_ready")
        s_st2 = sem("st2")
        s_mv2 = sem("mv2")
        s_ve2 = sem("ve2")
        s_rs2 = sem("rs2")
        s_xn2 = sem("xn2")
        s_tr2 = sem("tr2")
        s_xt2a = sem("xt2a")
        s_xt2b = sem("xt2b")
        s_x_hi = sem("x_hi")
        s_x_rest_hi = sem("x_rest_hi")
        s_x_parts = sem("x_parts")
        s_pg_done = sem("pg_done")
        s_gt_ready = sem("gt_ready")
        s_score_ready = sem("score_ready")
        s_biased_ready = sem("biased_ready")
        s_gsum_ready = sem("gsum_ready")
        s_ggt_ready = sem("ggt_ready")
        s_gge_ready = sem("gge_ready")
        s_gm_ready = sem("gm_ready")
        s_grank_ready = sem("grank_ready")
        s_gsel_ready = sem("gsel_ready")
        s_egt_ready = sem("egt_ready")
        s_ege_ready = sem("ege_ready")
        s_em_ready = sem("em_ready")
        s_ems_ready = sem("ems_ready")
        s_erank_ready = sem("erank_ready")
        s_esel_ready = sem("esel_ready")
        s_esel2_ready = sem("esel2_ready")
        s_ew_ready = sem("ew_ready")
        s_wsum_ready = sem("wsum_ready")
        s_weps_ready = sem("weps_ready")
        s_winv_ready = sem("winv_ready")
        s_cw_ready = sem("cw_ready")
        s_cwt_done = sem("cwt_done")
        s_cw_hi = sem("cw_hi")
        s_cw_r = sem("cw_r")
        s_cw_m = sem("cw_m")
        s_cw_mid = sem("cw_mid")
        s_cw_parts = sem("cw_parts")
        s_cw_spread = sem("cw_spread")
        s_e1_done = sem("e1_done")
        s_e3_done = sem("e3_done")
        s_et_ready = sem("et_ready")
        s_eq_ready = sem("eq_ready")
        s_eg_ready = sem("eg_ready")
        s_eh_ready = sem("eh_ready")
        s_e2_done = sem("e2_done")
        s_out_ready = sem("out_ready")
        s_out_stored = sem("out_stored")

        def wait(eng, sem, value):
            if isinstance(value, int) and value <= 0:
                return
            eng.wait_ge(sem, value)

        block = ctx.enter_context(nc.Block())
        ones, diag = yg[:, 0:P], yg[:, P:2 * P]
        A, B = slice(0, CH), slice(CH, PK)
        halves = [(slice(0, 64), slice(0, HALF)), (slice(64, 128), slice(HALF, CH))]

        def col(tile, name, part):
            i = 2 * COLS.index(name) + part
            return tile[:, i:i + 1]

        def images(ap):
            return ap.rearrange("p (m l) -> p m l", l=L)

        def bank_pair(i):
            return F[2 + i][:, 0:2 * D].rearrange("p (t d) -> p t d", d=D)

        def tok_tile(tt):
            return F[2 + tt // 2][:, (tt % 2) * D:(tt % 2) * D + D]

        W_EMBED = [(alphas, t["alphas"]), (tok_w, t["tok_w"])]
        W_MIXER = [(tok_b, t["tok_b"]), (ident, t["ident"]), (cols, t["cols"]), (in_w, t["in_w"]), (a_log, t["a_log"]), (delta_w, t["delta_w"]),
                   (bc_w, t["bc_w"]), (sel, t["sel"])]
        W_EXPERTS = [(w13_f32[0], t["w1"]), (w13_f32[1], t["w3"]), (w2, t["w2"])]
        W_POST = [(out_b, t["out_b"]), (out_w, t["out_w"]), (gate_w, t["gate_w"]), (gate_b, t["gate_b"]), (before4, t["before4"]),
                  (before8, t["before8"])]

        def over_chunks(eng, first, middle, last):
            first()
            with eng.Fori(0, (n_chunks - 2) // 2) as k:
                middle(k * 2 + 1, 1)
                middle(k * 2 + 2, 0)
            last()

        @block.sync
        def _(sp):
            def load_x(c):
                wait(sp, s_xq_top, 2 * c)
                sp.dma_start(xs[:], t["x"][c]).then_inc(s_x_in, 16)

            def store(c):
                sp.wait_ge(s_out_ready, c + 2)
                sp.dma_start(out[c], h1[:]).then_inc(s_out_stored, 16)

            sp.sem_inc(s_out_stored, 1)
            for tile, src in W_EMBED:
                sp.dma_start(tile[:], src).then_inc(s_w_embed, 16)
            load_x(0)
            for tile, src in W_MIXER:
                sp.dma_start(tile[:], src).then_inc(s_w_mixer, 16)
            for tile, src in W_EXPERTS:
                sp.dma_start(tile[:], src).then_inc(s_w_experts, 16)
            for tile, src in W_POST:
                sp.dma_start(tile[:], src).then_inc(s_w_post, 16)
            load_x(1)
            load_x(2)
            with sp.Fori(0, n_chunks - 3) as k:
                load_x(k + 3)
                store(k)
            sp.wait_ge(s_x_in, 16 * n_chunks)
            sp.sem_inc(s_x_in, 16)
            for c in range(n_chunks - 3, n_chunks):
                store(c)
            sp.wait_ge(s_out_stored, 16 * n_chunks + 1)

        @block.tensor
        def _(pe):
            mm = nc.tensor.matmul

            def project(dst_a, dst_b, w, m0, rhs_a, rhs_b):
                mm(dst_a, w[:, 0, m0:m0 + P], rhs_a, start=True, stop=False)
                mm(dst_a, w[0:DR, 1, m0:m0 + P], rhs_b, start=False, stop=True)
                for rows, toks in halves:
                    mm(dst_b[rows, :], w[:, 0, m0 + P:m0 + D], rhs_a[:, toks], start=True, stop=False)
                    last = mm(dst_b[rows, :], w[0:DR, 1, m0 + P:m0 + D], rhs_b[:, toks], start=False, stop=True)
                return last

            def remainder(dst, w, rhs, half):
                rows, toks = halves[half]
                return mm(dst[:, toks], w[rows, :], rhs[rows, B], start=False, stop=True,
                          skip_group_check=True)

            def turn(c, i, before):
                pe.wait_ge([s_xn1, s_xn2][i], c + 1)
                for sem, value in before:
                    wait(pe, sem, value)
                for tt in range(TT):
                    nc.tensor.transpose(F[0][:, tt * P:(tt + 1) * P], xn[i][:, tt, 0:P], ident[:])
                for tt in range(TT):
                    last = nc.tensor.transpose(F[1][0:DR, tt * P:(tt + 1) * P], xn[i][:, tt, P:D], ident[:])
                last.then_inc([s_tr1, s_tr2][i], 1)

            def embed(c):
                pe.wait_ge(s_xq_ready, 2 * (c + 1))
                wait(pe, s_out_ready, c - 1)
                wait(pe, s_bc_hi, c)
                wait(pe, s_bc_r, c)
                for tt in range(TT):
                    for k in range(KT):
                        last = mm(tok_tile(tt), xq[:, k * CH + tt * P:k * CH + (tt + 1) * P],
                                  tok_wq[:, k * D:(k + 1) * D], start=(k == 0), stop=(k == KT - 1))
                last.then_inc(s_conv_done, 1)

            def turn1(c):
                turn(c, 0, [(s_pd_read, c)])

            def in_x(c, post):
                pe.wait_ge(s_xt1a, c + 1)
                pe.wait_ge(s_xt1b, c + 1)
                pe.wait_ge(s_h0_ready, c + 1)
                if post:
                    pe.wait_ge(s_h1_ready, c - 1)
                project(F[2], F[3][:, 0:HALF], in_w, 0, xt[0], xtr[0][:]).then_inc(s_px_done, 1)

            def in_z(c):
                project(F[0], F[1][:, 0:HALF], in_w, D, xt[0], xtr[0][:]).then_inc(s_pz_done, 1)

            def delta_bc(c, par, step, post):
                x = xc[par]
                if step == 0:
                    pe.wait_ge(s_xc_ready, c + 1)
                    pe.wait_ge(s_zt_ready, c + 1)
                    pe.wait_ge(s_zh_ready, c + 1)
                    pe.wait_ge(s_cv0_ready, c + 1)
                    pe.wait_ge(s_xin_ready, c + 1)
                    if post:
                        pe.wait_ge(s_xt2a, c - 1)
                        pe.wait_ge(s_xt2b, c - 1)
                        pe.wait_ge(s_x_hi, c - 1)
                        pe.wait_ge(s_x_parts, 2 * (c - 1))
                    mm(F[2][0:96, :], bc_w[:, 0, :], x[:, A], start=True, stop=True)
                    remainder(F[2][0:96, :], bc_w[:, 1, :], x, 0)
                    mm(F[0], delta_w[:, 0, 0:P], x[:, A], start=True, stop=True)
                    remainder(F[0], delta_w[:, 1, 0:P], x, 0).then_inc(s_lower_rows, 1)
                    return
                for rows, toks in halves:
                    mm(F[1][rows, 0:HALF], delta_w[:, 0, P:D], x[:, toks], start=True, stop=False)
                    mm(F[1][rows, 0:HALF], delta_w[rows, 1, P:D], x[rows, B], start=False, stop=True)
                pe.wait_ge(s_lower_rows, c + 1)
                remainder(F[2][0:96, :], bc_w[:, 1, :], x, 1).then_inc(s_pbc_done, 1)
                remainder(F[0], delta_w[:, 1, 0:P], x, 1).then_inc(s_pd_done, 1)

            def spread(c, par, u):
                kind, n = UNITS[u]
                if u == 0:
                    pe.wait_ge(s_bc_ready, c + 1)
                for dst, row, free, before, sem in ((pb[u % 2], n, s_h_ready, u - 1, s_b_spread),
                                                    (pc, N + n, s_c_copied, u, s_c_spread)):
                    wait(pe, free, c * NU + before)
                    if kind == "A":
                        last = mm(dst[:], sel[:, row, :], bc[par][:, :], start=True, stop=True)
                    else:
                        for j in range(2):
                            for rows, toks in halves:
                                last = mm(dst[rows, j * HALF:(j + 1) * HALF], sel[:, row + j, 0:64],
                                          bc[par][:, toks], start=True, stop=True)
                    last.then_inc(sem, 1)

            def out_proj(c, pre):
                pe.wait_ge(s_yg_ready, 2 * (c + 1))
                pe.wait_ge(s_w_post, 16 * len(W_POST))
                if pre:
                    pe.wait_ge(s_h0_ready, c + 3)
                else:
                    pe.wait_ge(s_out_ready, c + 1)
                for tt in range(TT):
                    rows = halves[tt // 2][0]
                    b0 = CH + (tt % 2) * P
                    mm(tok_tile(tt), yg[:, tt * P:(tt + 1) * P], out_w[:, 0, :], start=True, stop=False)
                    last = mm(tok_tile(tt), yg[rows, b0:b0 + P], out_w[rows, 1, :], start=False, stop=True)
                last.then_inc(s_po_done, 1)

            def turn2(c, pre):
                turn(c, 1, [(s_zh_ready, c + 3), (s_zt_ready, c + 3)] if pre else [])

            def gate(c):
                pe.wait_ge(s_xt2a, c + 1)
                pe.wait_ge(s_xt2b, c + 1)
                for tt in range(TT):
                    dst = pw[:, tt * E:(tt + 1) * E]
                    mm(dst, xt[1][:, tt * P:(tt + 1) * P], gate_w[:, 0, :], start=True, stop=False)
                    last = mm(dst, xtr[1][:, tt * P:(tt + 1) * P], gate_w[0:DR, 1, :], start=False, stop=True)
                last.then_inc(s_pg_done, 1)

            def turn_cw(c):
                pe.wait_ge(s_cw_ready, c + 1)
                for tt in range(TT):
                    last = nc.tensor.transpose(pw[0:96, tt * P:(tt + 1) * P], cw3[:, tt, :, :].rearrange("p a b -> p (a b)"), ident[:])
                last.then_inc(s_cwt_done, 1)

            def spread_cw(c, e):
                if e == 0:
                    pe.wait_ge(s_cw_parts, c + 1)
                else:
                    pe.wait_ge(s_eh_ready, c * E + e)
                mm(pw[:], sel[:, e, :], cws[:, :], start=True, stop=True).then_inc(s_cw_spread, 1)

            def expert_up(c, k, pre):
                e = E if k == 0 else k - 1
                if k:
                    pe.wait_ge(s_eg_ready, c * EX + k)
                elif pre:
                    pe.wait_ge(s_pd_read, c + 3)
                if k == 0:
                    pe.wait_ge(s_w13_ready, 2)
                    pe.wait_ge(s_w2_ready, 1)
                    pe.wait_ge(s_x_parts, 2 * (c + 1))
                for dst, hi, lo, sem in ((F[0], w13_hi[0], w13_lo[0], s_e1_done),
                                         (F[1], w13_hi[1], w13_lo[1], s_e3_done)):
                    mm(dst, hi[:, 0, e, :], x_hi[:], start=True, stop=False)
                    mm(dst, hi[:, 0, e, :], x_lo[:], start=False, stop=False)
                    mm(dst, hi[:, 1, e, :], x_rest[:], start=False, stop=False)
                    mm(dst, lo[:, 0, e, :], x_hi[:], start=False, stop=False)
                    mm(dst, lo[0:DR, 1, e, :], x_rest[0:DR, :], start=False, stop=True).then_inc(sem, 1)

            def expert_down(c, k, pre):
                e = E if k == 0 else k - 1
                if k == 0 and pre:
                    pe.wait_ge(s_bc_r, c + 3)
                    pe.wait_ge(s_bc_hi, c + 3)
                if k == 0:
                    pe.wait_ge(s_eg_ready, c * EX + 1)
                else:
                    pe.wait_ge(s_eh_ready, c * E + k)
                for tt in range(TT):
                    last = mm(tok_tile(tt), eh[k % 2][:, tt * P:(tt + 1) * P], w2[:, e, :],
                              start=(k == 0 and tt % 2 == 0), stop=(k == EX - 1), skip_group_check=True)
                last.then_inc(s_e2_done, 1)

            def misc(slot, i, par, post, pre):
                steps = [name for name, at in PE_AT.items() if at == slot]
                if post:
                    c = i - 1
                    if "out_proj" in steps:
                        out_proj(c, pre)
                if pre:
                    c = i + 1
                    if "turn1" in steps:
                        turn1(c)
                    if "in_x" in steps:
                        in_x(c, post)
                    if "in_z" in steps:
                        in_z(c)
                if post:
                    c = i - 1
                    if "turn2" in steps:
                        turn2(c, pre)
                    if "gate" in steps:
                        gate(c)
                if pre:
                    c = i + 1
                    for step in range(2):
                        if f"delta{step}" in steps:
                            delta_bc(c, 1 - par, step, post)
                    if "embed" in steps:
                        embed(c + 1)
                if post:
                    c = i - 1
                    if "turn_cw" in steps:
                        turn_cw(c)
                    for k in range(EX):
                        if slot == UP[k]:
                            expert_up(c, k, pre)
                            if k:
                                spread_cw(c, k - 1)
                    for k in range(EX):
                        if slot == DOWN[k]:
                            expert_down(c, k, pre)

            def body(i, par, post=True, pre=True):
                for u in range(NU):
                    if u + 1 < NU:
                        spread(i, par, u + 1)
                    elif pre:
                        spread(i + 1, 1 - par, 0)
                    misc(u, i, par, post, pre)
                    if not post and u == 14:
                        spread_peak()

            def spread_peak():
                pe.wait_ge(s_peak_diag, 2)
                mm(pw[:, 0:P], ones, diag, start=True, stop=True).then_inc(s_peak_spread, 1)

            pe.wait_ge(s_prep, 1)
            embed(0)
            pe.wait_ge(s_w_mixer, 16 * len(W_MIXER))
            turn1(0)
            in_x(0, False)
            in_z(0)
            delta_bc(0, 0, 0, False)
            delta_bc(0, 0, 1, False)
            spread(0, 0, 0)
            embed(1)
            over_chunks(pe, lambda: body(0, 0, post=False), body, lambda: body(n_chunks - 1, 1, pre=False))
            c = n_chunks - 1
            out_proj(c, False)
            turn2(c, False)
            gate(c)
            expert_up(c, 0, False)
            turn_cw(c)
            for k in range(1, EX):
                expert_up(c, k, False)
                spread_cw(c, k - 1)
                expert_down(c, k - 1, False)
            expert_down(c, EX - 1, False)

        @block.scalar
        def _(act):
            f = nc.scalar.activation

            def scale_x(c, half):
                cols_ = slice(half * XH, (half + 1) * XH)
                act.wait_ge(s_x_in, (c + 1) * 16)
                f(xs[:, cols_], xs[:, cols_], ACT.Identity, bias=round_col[:], scale=inv_alpha[:, 0:1]).then_inc(s_x_scaled, 1)

            def norm_apply(c, i, src):
                act.wait_ge([s_rs1, s_rs2][i], c + 1)
                for tt in range(TT):
                    last = f(xn[i][:, tt, :], src[:, tt, :], ACT.Identity, bias=shift[i][:, tt:tt + 1],
                             scale=rstd[i][:, tt:tt + 1])
                last.then_inc([s_xn1, s_xn2][i], 1)

            def copy_turned(c, i):
                act.wait_ge([s_tr1, s_tr2][i], c + 1)
                if i == 1:
                    act.wait_ge(s_w13_ready, 2)
                f(xt[i], F[0], ACT.Copy).then_inc([s_xt1a, s_xt2a][i], 1)
                if i == 0:
                    f(xtr[i][:], F[1][0:DR, :], ACT.Copy).then_inc(s_xt1b, 1)

            def x_evac(c):
                act.wait_ge(s_px_done, c + 1)
                wait(act, s_cv2_ready, c * 2)
                for part, (dst, src) in enumerate(((A, F[2]), (B, F[3][:, 0:HALF]))):
                    last = f(xin[:, dst], src, ACT.Identity, bias=col(cols, "in_b_x", part))
                last.then_inc(s_xin_ready, 1)
                wait(act, s_xc_ready, c)
                for part, (dst, src) in enumerate(((A, F[2]), (B, F[3][:, 0:HALF]))):
                    last = f(cv[:, dst], src, ACT.Identity, bias=conv_bias[:, part:part + 1],
                             scale=col(col_half, "conv_w1", part))
                last.then_inc(s_cv0_ready, 1)

            def z_evac(c):
                act.wait_ge(s_pz_done, c + 1)
                wait(act, s_zs_ready, c)
                wait(act, s_dt_ready, c)
                srcs = ((A, F[0]), (B, F[1][:, 0:HALF]))
                for part, (dst, src) in enumerate(srcs):
                    last = f(zh[:, dst], src, ACT.Identity, bias=col(col_half, "in_b_z", part), scale=0.5)
                last.then_inc(s_zh_ready, 1)
                for part, (dst, src) in enumerate(srcs):
                    last = f(zt[:, dst], src, ACT.Tanh, bias=col(col_half, "in_b_z", part), scale=0.5)
                last.then_inc(s_zt_ready, 1)

            def conv_tanh(c):
                act.wait_ge(s_cv2_ready, (c + 1) * 2)
                wait(act, s_dt_ready, c)
                f(cvt[:], cv[:], ACT.Tanh).then_inc(s_cvt_ready, 1)

            def delta_evac(c):
                act.wait_ge(s_pd_done, c + 1)
                wait(act, s_dt_ready, c)
                for part, (dst, src) in enumerate(((A, F[0]), (B, F[1][:, 0:HALF]))):
                    last = f(sp_ln[:, dst], src, ACT.Identity, bias=col(cols, "delta_b", part))
                last.then_inc(s_pd_read, 1)

            def softplus(c, step):
                if step == "relu":
                    act.wait_ge(s_pd_read, c + 1)
                    act.wait_ge(s_zs_ready, c + 1)
                    f(sp_relu[:], sp_ln[:], ACT.Relu).then_inc(s_relu_ready, 1)
                if step == "abs":
                    act.wait_ge(s_relu_ready, c + 1)
                    f(sp_ln[:], sp_ln[:], ACT.Abs).then_inc(s_abs_ready, 1)
                if step == "exp":
                    act.wait_ge(s_abs_ready, c + 1)
                    f(sp_ln[:], sp_ln[:], ACT.Exp, scale=-1.0).then_inc(s_spe_ready, 1)
                if step == "ln":
                    act.wait_ge(s_spe_ready, c + 1)
                    f(sp_ln[:], sp_ln[:], ACT.Ln, bias=1.0).then_inc(s_spl_ready, 1)

            def y_init(c, par):
                act.wait_ge(s_xc_ready, c + 1)
                wait(act, s_yg_ready, 2 * (c - 1))
                f(ya[par][:, 0:CH], xc[par][:, A], ACT.Copy, scale=col(cols, "D_param", 0))
                f(ya[par][:, CH:].rearrange("p (j m) -> p j m", j=2),
                  xc[par][:, B].unsqueeze(1).broadcast_to([P, 2, HALF]), ACT.Copy,
                  scale=col(col_half, "D_param", 1)).then_inc(s_y_init, 1)

            def bc_high(c, par):
                act.wait_ge(s_pbc_done, c + 1)
                wait(act, s_c_spread, (c - 1) * NU)
                f(bc[par][:, :], F[2][0:96, :], ACT.Copy).then_inc(s_bc_hi, 1)

            def decays(c, par, u):
                kind, n = UNITS[u]
                if u == 0:
                    act.wait_ge(s_dt_ready, c + 1)
                wait(act, s_h_ready, c * NU + u - A_RING + 1)
                dst = images(decay[u % A_RING])
                src = images(dt[par][:])
                if kind == "A":
                    f(dst[:, :, 1:L], src[:, 0:8, 1:L], ACT.Exp, scale=a_neg[:, n:n + 1]).then_inc(s_decay_ready, 1)
                else:
                    for j in range(2):
                        last = f(dst[:, 4 * j:4 * j + 4, 1:L], src[:, 8:12, 1:L], ACT.Exp,
                                 scale=a_neg[:, N + n + j:N + n + j + 1])
                    last.then_inc(s_decay_ready, 1)

            def copy_c(c, u):
                act.wait_ge(s_c_spread, c * NU + u + 1)
                wait(act, s_hc_ready, c * NU + u - C_RING + 1)
                f(cs[u % C_RING], pc[:], ACT.Copy).then_inc(s_c_copied, 1)

            def gate_tanh(c):
                act.wait_ge(s_pg_done, c + 1)
                f(gt[:], pw[:, 0:TT * E], ACT.Tanh, scale=0.5).then_inc(s_gt_ready, 1)

            def cw_high(c):
                act.wait_ge(s_cwt_done, c + 1)
                f(cws[:, :], pw[0:96, :], ACT.Copy).then_inc(s_cw_hi, 1)

            def x_high(c):
                act.wait_ge(s_tr2, c + 1)
                f(x_hi[:], F[0], ACT.Copy).then_inc(s_x_hi, 1)
                act.wait_ge(s_xt2b, c + 1)
                f(x_rest[0:DR, :], F[1][0:DR, :], ACT.Copy).then_inc(s_x_rest_hi, 1)

            def expert_tanh(c, k):
                act.wait_ge(s_e1_done, c * EX + k + 1)
                if k:
                    act.wait_ge(s_eq_ready, c * EX + k)
                f(et, F[0], ACT.Tanh, scale=half_unscale[:, 0:1]).then_inc(s_et_ready, 1)

            def misc(slot, i, par, post, pre):
                steps = [name for name, at in ACT_AT.items() if at == slot]
                if pre:
                    c = i + 1
                    if "norm_apply1" in steps:
                        norm_apply(c, 0, h0[1 - par])
                    if "copy1" in steps:
                        copy_turned(c, 0)
                    if "x_evac" in steps:
                        x_evac(c)
                    if "z_evac" in steps:
                        z_evac(c)
                    if "conv_tanh" in steps:
                        conv_tanh(c)
                    if "delta_evac" in steps:
                        delta_evac(c)
                    if "bc_high" in steps:
                        bc_high(c, 1 - par)
                    if "y_init" in steps:
                        y_init(c, 1 - par)
                    for half in range(2):
                        if f"scale_x{half}" in steps:
                            scale_x(c + 1, half)
                    for step in ("relu", "abs", "exp", "ln"):
                        if step in steps:
                            softplus(c, step)
                if post:
                    c = i - 1
                    if "norm_apply2" in steps:
                        norm_apply(c, 1, h1)
                    if "copy2" in steps:
                        copy_turned(c, 1)
                        x_high(c)
                    if "gate_tanh" in steps:
                        gate_tanh(c)
                    if "cw_high" in steps:
                        cw_high(c)
                    for k in range(EX):
                        if slot == UP[k]:
                            expert_tanh(c, k)

            def body(i, par, post=True, pre=True):
                for u in range(NU):
                    if u + 1 < NU:
                        decays(i, par, u + 1)
                    elif pre:
                        decays(i + 1, 1 - par, 0)
                    if u + 1 < NU:
                        copy_c(i, u + 1)
                    elif pre:
                        copy_c(i + 1, 0)
                    misc(u, i, par, post, pre)
                    if not post and u in (16, 18):
                        expert_weights((u - 16) // 2)

            def expert_weights(i):
                act.wait_ge(s_scale_ready, 1)
                f(w13_f32[i], w13_f32[i], ACT.Copy, scale=w_scale[:, 0:1]).then_inc(s_w13_scaled, 1)
                act.wait_ge(s_w13_scaled, i + 1)
                f(w13_hi[i][:], w13_f32[i], ACT.Copy).then_inc(s_w13_hi, 1)

            act.wait_ge(s_cols_ready, 1)
            scale_x(0, 0)
            scale_x(0, 1)
            act.wait_ge(s_w_mixer, 16 * len(W_MIXER))
            f(a_neg[:], a_log[:], ACT.Exp).then_inc(s_avec_exp, 1)
            norm_apply(0, 0, h0[0])
            copy_turned(0, 0)
            act.wait_ge(s_mixer_prep, 1)
            x_evac(0)
            conv_tanh(0)
            z_evac(0)
            scale_x(1, 0)
            scale_x(1, 1)
            delta_evac(0)
            bc_high(0, 0)
            for step in ("relu", "abs", "exp", "ln"):
                softplus(0, step)
            decays(0, 0, 0)
            y_init(0, 0)
            copy_c(0, 0)
            over_chunks(act, lambda: body(0, 0, post=False), body, lambda: body(n_chunks - 1, 1, pre=False))
            c = n_chunks - 1
            norm_apply(c, 1, h1)
            copy_turned(c, 1)
            x_high(c)
            gate_tanh(c)
            expert_tanh(c, 0)
            cw_high(c)
            for k in range(1, EX):
                expert_tanh(c, k)

        @block.vector
        def _(dve):
            v = nc.vector

            def quantise(c, half):
                cols_ = slice(half * XH, (half + 1) * XH)
                dve.wait_ge(s_x_scaled, 2 * c + half + 1)
                wait(dve, s_conv_done, c)
                v.tensor_scalar(xq[:, cols_], xs[:, cols_], ROUND, 127.0, ALU.subtract, ALU.min).then_inc(s_xq_top, 1)
                dve.wait_ge(s_xq_top, 2 * c + half + 1)
                v.tensor_scalar(xq[:, cols_], xq[:, cols_], -128.0, None, ALU.max).then_inc(s_xq_ready, 1)

            def embed_out(c, par):
                dve.wait_ge(s_conv_done, c + 1)
                wait(dve, s_h0b_ready, c - 1)
                for i in range(2):
                    dst = h0[par][:, 2 * i:2 * i + 2, :].rearrange("p t d -> p (t d)")
                    last = v.scalar_tensor_tensor(dst, F[2 + i][:, 0:2 * D], alpha_prod[:, 0:1], tok_b[:],
                                                  ALU.mult, ALU.add)
                last.then_inc(s_h0_ready, 1)

            def norm_stats(c, i, src, src_sem):
                st_sem, mv_sem, ve_sem = [(s_st1, s_mv1, s_ve1), (s_st2, s_mv2, s_ve2)][i]
                dve.wait_ge(src_sem, c + 1)
                for tt in range(TT):
                    last = v.bn_stats(stats[i][:, tt, :], src[:, tt, :])
                last.then_inc(st_sem, 1)
                dve.wait_ge(st_sem, c + 1)
                dve.sem_inc(s_stats_seen, 1)
                for tt in range(TT):
                    last = v.bn_aggr(mv[i][:, tt, :], stats[i][:, tt, :])
                last.then_inc(mv_sem, 1)
                dve.wait_ge(mv_sem, c + 1)
                v.tensor_scalar(neg_mean[i][:], mv[i][:, :, 0], -1.0, None, ALU.mult).then_inc([s_nm1, s_nm2][i], 1)
                v.tensor_scalar(vare[i][:], mv[i][:, :, 1], LN_EPS, None, ALU.add).then_inc(ve_sem, 1)

            def x_low(c):
                dve.wait_ge(s_x_hi, c + 1)
                v.tensor_tensor(x_lo[:], F[0], x_hi[:], ALU.subtract).then_inc(s_x_parts, 1)
                dve.wait_ge(s_x_rest_hi, c + 1)
                v.tensor_tensor(x_rest[DR:2 * DR, :], F[1][0:DR, :], x_rest[0:DR, :], ALU.subtract)\
                    .then_inc(s_x_parts, 1)

            def copy_turned(c):
                dve.wait_ge(s_tr2, c + 1)
                v.tensor_copy(xtr[1][:], F[1][0:DR, :]).then_inc(s_xt2b, 1)

            def conv(c):
                dve.wait_ge(s_xin_ready, c + 1)
                dve.wait_ge(s_cv0_ready, c + 1)
                for name, dst_l, src_l, done in (("conv_w0", slice(1, L), slice(0, L - 1), s_cv1_ready),
                                                 ("conv_w2", slice(0, L - 1), slice(1, L), s_cv2_ready)):
                    for part, cols_ in enumerate((A, B)):
                        o = images(cv[:, cols_])[:, :, dst_l]
                        ins = v.scalar_tensor_tensor(o, images(xin[:, cols_])[:, :, src_l],
                                                     col(col_half, name, part), o, ALU.mult, ALU.add)
                        ins.then_inc(done, 1)
                    if done is s_cv1_ready:
                        dve.wait_ge(s_cv1_ready, (c + 1) * 2)

            def conv_gate(c, par):
                dve.wait_ge(s_cvt_ready, c + 1)
                wait(dve, s_y_init, c - 1)
                v.scalar_tensor_tensor(xc[par][:], cvt[:], 1.0, cv[:], ALU.add, ALU.mult).then_inc(s_xc_ready, 1)

            def z_gate(c, par):
                dve.wait_ge(s_zt_ready, c + 1)
                dve.wait_ge(s_zh_ready, c + 1)
                wait(dve, s_yg_ready, 2 * (c - 1))
                v.scalar_tensor_tensor(zs[par][:], zt[:], 1.0, zh[:], ALU.add, ALU.mult).then_inc(s_zs_ready, 1)

            def split(c, src, hi, r, m, sems, step):
                hi_sem, r_sem, m_sem, mid_sem, done = sems
                if step == 0:
                    dve.wait_ge(hi_sem, c + 1)
                    v.tensor_tensor(r[:], src, hi[:], ALU.subtract).then_inc(r_sem, 1)
                    return
                dve.wait_ge(r_sem, c + 1)
                v.tensor_copy(m[:], r[:]).then_inc(m_sem, 1)
                dve.wait_ge(m_sem, c + 1)
                v.tensor_copy(hi[32:64, :], m[32:64, :]).then_inc(mid_sem, 1)
                dve.wait_ge(mid_sem, c + 1)
                v.tensor_tensor(hi[64:96, :], r[64:96, :], m[64:96, :], ALU.subtract).then_inc(done, 1)

            def split_bc(c, par, step):
                split(c, F[2][0:96, :], bc[par], split_r, split_m, (s_bc_hi, s_bc_r, s_bc_m, s_bc_mid, s_bc_ready), step)

            def split_cw(c, step):
                split(c, pw[0:96, :], cws, csplit_r, csplit_m, (s_cw_hi, s_cw_r, s_cw_m, s_cw_mid, s_cw_parts), step)

            def step_sizes(c, par):
                dve.wait_ge(s_relu_ready, c + 1)
                dve.wait_ge(s_spl_ready, c + 1)
                wait(dve, s_decay_ready, (c - 1) * NU)
                v.tensor_tensor(dt[par][:], sp_relu[:], sp_ln[:], ALU.add).then_inc(s_dt_ready, 1)
                dve.wait_ge(s_dt_ready, c + 1)
                wait(dve, s_b_times_u, (c - 1) * NU)
                v.tensor_tensor(ut[par][:], dt[par][:], xc[par][:], ALU.mult).then_inc(s_ut_ready, 1)

            def scan(c, par, u):
                kind, n = UNITS[u]
                b = pb[u % 2]
                if u == 0:
                    dve.wait_ge(s_ut_ready, c + 1)
                dve.wait_ge(s_b_spread, c * NU + u + 1)
                if kind == "A":
                    v.tensor_tensor(b[:], b[:], ut[par][:, A], ALU.mult).then_inc(s_b_times_u, 1)
                else:
                    two = b[:].rearrange("p (j m) -> p j m", j=2)
                    v.tensor_tensor(two, two, ut[par][:, B].unsqueeze(1).broadcast_to([P, 2, HALF]),
                                    ALU.mult).then_inc(s_b_times_u, 1)
                dve.wait_ge(s_decay_ready, c * NU + u + 1)
                wait(dve, s_hc_ready, c * NU + u - H_RING + 1)
                dve.wait_ge(s_b_times_u, c * NU + u + 1)
                v.tensor_tensor_scan(hs[u % H_RING], decay[u % A_RING], b[:], 0.0,
                                     ALU.mult, ALU.add).then_inc(s_h_ready, 1)

            def mixer_out(c, par):
                dve.wait_ge(s_y_added, (c + 1) * NU)
                v.tensor_tensor(yb[:], ya[par][:, CH:CH + HALF], ya[par][:, CH + HALF:], ALU.add)\
                    .then_inc(s_yb_ready, 1)
                v.tensor_tensor(yg[:, A], ya[par][:, A], zs[par][:, A], ALU.mult).then_inc(s_yg_ready, 1)
                dve.wait_ge(s_yb_ready, c + 1)
                v.tensor_tensor(yg[:, B], yb[:], zs[par][:, B], ALU.mult).then_inc(s_yg_ready, 1)

            def residual(c):
                dve.wait_ge(s_po_done, c + 1)
                dve.wait_ge(s_h0b_ready, c + 1)
                dve.wait_ge(s_out_stored, c * 16 + 1)
                for i in range(2):
                    last = v.tensor_tensor(h1[:, 2 * i:2 * i + 2, :], bank_pair(i), h0b[:, 2 * i:2 * i + 2, :], ALU.add)
                last.then_inc(s_h1_ready, 1)

            def beats(c, gt_, ge_, values, n, before, sems, keep=None):
                gt_sem, ge_sem, m_sem = sems
                other = values.unsqueeze(2).broadcast_to([P, TT, n, n])
                own = values.unsqueeze(3).broadcast_to([P, TT, n, n])
                lower = before[:].rearrange("p (a b) -> p a b", a=n).unsqueeze(1).broadcast_to([P, TT, n, n])
                v.tensor_tensor(gt_[:], other, own, ALU.is_gt).then_inc(gt_sem, 1)
                v.tensor_tensor(ge_[:], other, own, ALU.is_ge).then_inc(ge_sem, 1)
                dve.wait_ge(ge_sem, 2 * c + 1)
                v.tensor_tensor(ge_[:], ge_[:], lower, ALU.mult).then_inc(ge_sem, 1)
                dve.wait_ge(ge_sem, 2 * c + 2)
                dve.wait_ge(gt_sem, c + 1)
                v.tensor_tensor(gt_[:], gt_[:], ge_[:], ALU.max).then_inc(m_sem, 1)
                dve.wait_ge(m_sem, c + 1)

            def route_groups(c):
                dve.wait_ge(s_gt_ready, c + 1)
                dve.wait_ge(s_w_post, 16 * len(W_POST))
                v.tensor_scalar(score[:].rearrange("p t e -> p (t e)"), gt[:], 0.5, 0.5, ALU.mult,
                                ALU.add).then_inc(s_score_ready, 1)
                dve.wait_ge(s_score_ready, c + 1)
                v.tensor_tensor(biased[:], score[:], gate_b[:].rearrange("p (t e) -> p t e", e=E),
                                ALU.add).then_inc(s_biased_ready, 1)
                dve.wait_ge(s_biased_ready, c + 1)
                pairs = biased[:].rearrange("p t (g j) -> p t g j", j=2)
                v.tensor_tensor(gsum[:], pairs[:, :, :, 0], pairs[:, :, :, 1], ALU.add).then_inc(s_gsum_ready, 1)
                dve.wait_ge(s_gsum_ready, c + 1)
                beats(c, g_gt, g_ge, gsum[:], 4, before4, (s_ggt_ready, s_gge_ready, s_gm_ready))
                v.tensor_reduce(g_rank[:], g_gt[:], AX.X, ALU.add).then_inc(s_grank_ready, 1)
                dve.wait_ge(s_grank_ready, c + 1)
                v.tensor_scalar(g_sel[:], g_rank[:], 2.0, None, ALU.is_lt).then_inc(s_gsel_ready, 1)

            def route_experts(c):
                dve.wait_ge(s_gsel_ready, c + 1)
                beats(c, e_gt, e_ge, biased[:], 8, before8, (s_egt_ready, s_ege_ready, s_em_ready))
                sel_b = g_sel[:].unsqueeze(3).broadcast_to([P, TT, 4, 2])
                v.tensor_copy(e_sel[:].rearrange("p t (g j) -> p t g j", j=2), sel_b).then_inc(s_esel_ready, 1)
                dve.wait_ge(s_esel_ready, c + 1)
                v.tensor_tensor(e_gt[:], e_gt[:], e_sel[:].unsqueeze(2).broadcast_to([P, TT, 8, 8]),
                                ALU.mult).then_inc(s_ems_ready, 1)
                dve.wait_ge(s_ems_ready, c + 1)
                v.tensor_reduce(e_rank[:], e_gt[:], AX.X, ALU.add).then_inc(s_erank_ready, 1)
                dve.wait_ge(s_erank_ready, c + 1)
                v.scalar_tensor_tensor(e_sel[:], e_rank[:], 2.0, e_sel[:], ALU.is_lt, ALU.mult)\
                    .then_inc(s_esel2_ready, 1)
                dve.wait_ge(s_esel2_ready, c + 1)
                v.tensor_tensor(e_w[:], e_sel[:], score[:], ALU.mult).then_inc(s_ew_ready, 1)
                dve.wait_ge(s_ew_ready, c + 1)
                v.tensor_reduce(wsum[:], e_w[:], AX.X, ALU.add).then_inc(s_wsum_ready, 1)
                dve.wait_ge(s_wsum_ready, c + 1)
                v.tensor_scalar(wsum[:], wsum[:], 1e-6, None, ALU.add).then_inc(s_weps_ready, 1)
                dve.wait_ge(s_weps_ready, c + 1)
                v.reciprocal(winv[:], wsum[:]).then_inc(s_winv_ready, 1)
                dve.wait_ge(s_winv_ready, c + 1)
                for copy in range(3):
                    last = v.tensor_tensor(cw3[:, :, copy, 0:E], e_w[:], winv[:].unsqueeze(2).broadcast_to([P, TT, E]),
                                           ALU.mult)
                last.then_inc(s_cw_ready, 1)

            def expert_mul(c, k):
                dve.wait_ge(s_et_ready, c * EX + k + 1)
                if k:
                    dve.wait_ge(s_eg_ready, c * EX + k)
                v.scalar_tensor_tensor(eq, et, 1.0, F[0], ALU.add, ALU.mult).then_inc(s_eq_ready, 1)
                dve.wait_ge(s_e3_done, c * EX + k + 1)
                dve.wait_ge(s_eq_ready, c * EX + k + 1)
                v.tensor_tensor(eg if k else eh[0], eq, F[1], ALU.mult).then_inc(s_eg_ready, 1)
                if k:
                    dve.wait_ge(s_eg_ready, c * EX + k + 1)
                    dve.wait_ge(s_cw_spread, c * E + k)
                    if k >= 2:
                        dve.wait_ge(s_e2_done, c * EX + k - 1)
                    v.tensor_tensor(eh[k % 2], eg, pw[:], ALU.mult).then_inc(s_eh_ready, 1)

            def finish(c):
                dve.wait_ge(s_e2_done, (c + 1) * EX)
                for i in range(2):
                    last = v.tensor_tensor(h1[:, 2 * i:2 * i + 2, :], bank_pair(i), h1[:, 2 * i:2 * i + 2, :], ALU.add)
                last.then_inc(s_out_ready, 1)

            def misc(slot, i, par, post, pre):
                steps = [name for name, at in DVE_AT.items() if at == slot]
                if post:
                    c = i - 1
                    if "mixer_out" in steps:
                        mixer_out(c, 1 - par)
                if pre:
                    c = i + 1
                    if "embed_out" in steps:
                        embed_out(c, 1 - par)
                    if "stats1" in steps:
                        norm_stats(c, 0, h0[1 - par], s_h0_ready)
                if post:
                    c = i - 1
                    if "residual" in steps:
                        residual(c)
                    if "stats2" in steps:
                        norm_stats(c, 1, h1, s_h1_ready)
                if pre:
                    c = i + 1
                    if "conv" in steps:
                        conv(c)
                    if "conv_gate" in steps:
                        conv_gate(c, 1 - par)
                    if "z_gate" in steps:
                        z_gate(c, 1 - par)
                if post:
                    c = i - 1
                    if "copy2" in steps:
                        copy_turned(c)
                    if "x_low" in steps:
                        x_low(c)
                    if "route_groups" in steps:
                        route_groups(c)
                    if "route_experts" in steps:
                        route_experts(c)
                    if "cw_rest" in steps:
                        split_cw(c, 0)
                    if "cw_parts" in steps:
                        split_cw(c, 1)
                if pre:
                    c = i + 1
                    if "bc_rest" in steps:
                        split_bc(c, 1 - par, 0)
                    if "bc_parts" in steps:
                        split_bc(c, 1 - par, 1)
                    for half in range(2):
                        if f"quantise{half}" in steps:
                            quantise(c + 1, half)
                    if "step_sizes" in steps:
                        step_sizes(c, 1 - par)
                if post:
                    c = i - 1
                    if slot == UP[0]:
                        expert_mul(c, 0)
                    for k in range(1, EX):
                        if slot == UP[k]:
                            expert_mul(c, k)
                    if "finish" in steps:
                        finish(c)

            def expert_peak(step):
                if step == 0:
                    dve.wait_ge(s_w_experts, 16 * len(W_EXPERTS))
                    v.tensor_reduce(w_peak[:, 0:1], w13, AX.X, ALU.max)
                    return
                v.tensor_reduce(w_peak[:, 1:2], w13, AX.X, ALU.min).then_inc(s_peak_in, 1)
                dve.wait_ge(s_peak_in, 1)
                v.tensor_scalar(w_peak[:, 2:3], w_peak[:, 1:2], -1.0, None, ALU.mult).then_inc(s_peak_in, 1)
                dve.wait_ge(s_peak_in, 2)
                v.tensor_tensor(w_peak[:, 3:4], w_peak[:, 0:1], w_peak[:, 2:3], ALU.max).then_inc(s_peak_ready, 1)
                dve.wait_ge(s_peak_ready, 1)
                v.tensor_scalar(diag, ident[:], w_peak[:, 3:4], None, ALU.mult).then_inc(s_peak_diag, 2)

            def expert_scale():
                dve.wait_ge(s_peak_spread, 1)
                v.tensor_reduce(w_peak[:, 0:1], pw[:, 0:P], AX.X, ALU.max).then_inc(s_peak_all, 1)
                dve.wait_ge(s_peak_all, 1)
                v.tensor_scalar(w_peak[:, 1:2], w_peak[:, 0:1], 2.0 ** -80, 2.0 ** 80, ALU.max, ALU.min)\
                    .then_inc(s_peak_all, 1)
                dve.wait_ge(s_peak_all, 2)
                v.tensor_scalar(w_peak[:, 2:3].bitcast(I32), w_peak[:, 1:2].bitcast(I32), EXPONENT, None,
                                ALU.bitwise_and).then_inc(s_peak_all, 1)
                dve.wait_ge(s_peak_all, 3)
                v.tensor_scalar(w_peak[:, 3:4].bitcast(I32), w_peak[:, 2:3].bitcast(I32), -1.0, float(254 << 23),
                                ALU.mult, ALU.add).then_inc(s_peak_all, 1)
                dve.wait_ge(s_peak_all, 4)
                v.tensor_scalar(w_scale[:], w_peak[:, 3:4], W_TOP, None, ALU.mult)
                v.tensor_scalar(w_unscale[:], w_peak[:, 2:3], 1 / W_TOP, None, ALU.mult).then_inc(s_scale_ready, 1)
                dve.wait_ge(s_scale_ready, 1)
                v.tensor_scalar(half_unscale[:], w_unscale[:], 0.5, None, ALU.mult).then_inc(s_peak_all, 1)
                dve.wait_ge(s_peak_all, 5)
                v.tensor_scalar(w2[:].rearrange("p e d -> p (e d)"), w2[:].rearrange("p e d -> p (e d)"),
                                w_unscale[:, 0:1], half_unscale[:, 0:1], ALU.mult, ALU.mult).then_inc(s_w2_ready, 1)

            def body(i, par, post=True, pre=True):
                for u in range(NU):
                    scan(i, par, u)
                    misc(u, i, par, post, pre)
                    if not post and u in (9, 11):
                        expert_peak((u - 9) // 2)
                    if not post and u == 15:
                        expert_scale()

            v.memset(round_col[:], ROUND)
            v.memset(neg_half[:], -0.5).then_inc(s_out_ready, 1)
            v.memset(cw3[:].rearrange("p a b c -> p (a b c)"), 0.0)
            v.memset(ones, 1.0)
            for i in range(A_RING):
                v.memset(decay[i], 0.0)
            dve.wait_ge(s_w_embed, 16 * len(W_EMBED))
            v.tensor_tensor(alpha_prod[:], alphas[:, 0:1], alphas[:, 1:2], ALU.mult)
            v.reciprocal(inv_alpha[:], alphas[:]).then_inc(s_cols_ready, 1)
            dve.wait_ge(s_cols_ready, 1)
            v.tensor_scalar(tok_w[:], tok_w[:], inv_alpha[:, 1:2], ROUND, ALU.mult, ALU.add).then_inc(s_tokw_scaled, 1)
            dve.wait_ge(s_tokw_scaled, 1)
            v.tensor_scalar(tok_w[:], tok_w[:], ROUND, 127.0, ALU.subtract, ALU.min).then_inc(s_tokw_clamped, 1)
            dve.wait_ge(s_tokw_clamped, 1)
            v.tensor_scalar(tok_wq[:], tok_w[:], -128.0, None, ALU.max).then_inc(s_prep, 1)
            quantise(0, 0)
            quantise(0, 1)
            dve.wait_ge(s_w_mixer, 16 * len(W_MIXER))
            v.tensor_scalar(col_half[:], cols[:], 0.5, None, ALU.mult).then_inc(s_consts, 1)
            dve.wait_ge(s_consts, 1)
            ib, cw1, cb = (2 * COLS.index(n) for n in ("in_b_x", "conv_w1", "conv_b"))
            v.tensor_tensor(conv_bias[:], cols[:, ib:ib + 2], col_half[:, cw1:cw1 + 2], ALU.mult).then_inc(s_consts, 1)
            dve.wait_ge(s_consts, 2)
            v.tensor_tensor(conv_bias[:], conv_bias[:], col_half[:, cb:cb + 2], ALU.add).then_inc(s_mixer_prep, 1)
            dve.wait_ge(s_avec_exp, 1)
            v.tensor_scalar(a_neg[:], a_neg[:], -1.0, None, ALU.mult).then_inc(s_avec_ready, 1)
            embed_out(0, 0)
            norm_stats(0, 0, h0[0], s_h0_ready)
            conv(0)
            conv_gate(0, 0)
            z_gate(0, 0)
            quantise(1, 0)
            quantise(1, 1)
            split_bc(0, 0, 0)
            split_bc(0, 0, 1)
            step_sizes(0, 0)
            over_chunks(dve, lambda: body(0, 0, post=False), body, lambda: body(n_chunks - 1, 1, pre=False))
            c = n_chunks - 1
            mixer_out(c, 1)
            residual(c)
            norm_stats(c, 1, h1, s_h1_ready)
            copy_turned(c)
            x_low(c)
            route_groups(c)
            route_experts(c)
            expert_mul(c, 0)
            split_cw(c, 0)
            split_cw(c, 1)
            for k in range(1, EX):
                expert_mul(c, k)
            finish(c)

        @block.gpsimd
        def _(pool):
            g = nc.gpsimd

            def inv_std(c, i):
                ve_sem, nm_sem, pow_sem, rs_sem = [(s_ve1, s_nm1, s_pow1, s_rs1), (s_ve2, s_nm2, s_pow2, s_rs2)][i]
                pool.wait_ge(ve_sem, c + 1)
                g.tensor_tensor(rstd[i][:], vare[i][:], neg_half[:], ALU.pow).then_inc(pow_sem, 1)
                pool.wait_ge(pow_sem, c + 1)
                pool.wait_ge(nm_sem, c + 1)
                g.tensor_tensor(shift[i][:], neg_mean[i][:], rstd[i][:], ALU.mult).then_inc(rs_sem, 1)

            def with_out_b(c, par):
                pool.wait_ge(s_h0_ready, c + 1)
                wait(pool, s_h1_ready, c)
                pool.wait_ge(s_w_post, 16 * len(W_POST))
                flat = "p t d -> p (t d)"
                g.tensor_tensor(h0b[:].rearrange(flat), h0[par][:].rearrange(flat), out_b[:], ALU.add)\
                    .then_inc(s_h0b_ready, 1)

            def times_c(c, u):
                pool.wait_ge(s_h_ready, c * NU + u + 1)
                pool.wait_ge(s_c_copied, c * NU + u + 1)
                wait(pool, s_y_added, c * NU + u - Y_RING + 1)
                g.tensor_tensor(hc[u % Y_RING], hs[u % H_RING], cs[u % C_RING], ALU.mult).then_inc(s_hc_ready, 1)

            def add_y(c, par, u):
                pool.wait_ge(s_hc_ready, c * NU + u + 1)
                if u == 0:
                    pool.wait_ge(s_y_init, c + 1)
                wait(pool, s_y_added, c * NU + u)
                dst = ya[par][:, 0:CH] if UNITS[u][0] == "A" else ya[par][:, CH:2 * CH]
                g.tensor_tensor(dst, dst, hc[u % Y_RING], ALU.add).then_inc(s_y_added, 1)

            def misc(slot, i, par, post, pre):
                if pre and slot == POOL_AT["inv_std1"]:
                    inv_std(i + 1, 0)
                if post:
                    c = i - 1
                    if slot == POOL_AT["inv_std2"]:
                        inv_std(c, 1)

            def body(i, par, post=True, pre=True):
                for u in range(NU):
                    times_c(i, u)
                    add_y(i, par, u)
                    misc(u, i, par, post, pre)
                    if u == POOL_AT["with_out_b"]:
                        with_out_b(i, par)
                    if not post and u in (18, 20):
                        expert_weights((u - 18) // 2)

            def expert_weights(i):
                pool.wait_ge(s_w13_hi, i + 1)
                g.tensor_tensor(w13_lo[i][:], w13_f32[i], w13_hi[i][:], ALU.subtract).then_inc(s_w13_ready, 1)

            inv_std(0, 0)
            over_chunks(pool, lambda: body(0, 0, post=False), body, lambda: body(n_chunks - 1, 1, pre=False))
            inv_std(n_chunks - 1, 1)


def kernel(**inputs):
    import numpy as np
    import ml_dtypes
    import concourse.bacc as bacc
    from concourse.bass_utils import run_bass_kernel_spmd

    a = {k: np.asarray(v) for k, v in inputs.items()}
    f32 = np.float32

    def twice(m):
        return np.stack([m[:P], np.concatenate([m[P:], m[P:]])], axis=1)

    def on_all(v):
        return np.broadcast_to(np.ravel(v), (P, np.size(v)))

    n_img = a["x"].shape[0]
    n_chunks = n_img * L // CH
    x = a["x"].reshape(n_chunks, CH // L, 3, 8, 16, 8, 16).transpose(0, 2, 4, 6, 1, 3, 5)
    x = x.reshape(n_chunks, KT, P, CH).transpose(0, 2, 1, 3).reshape(n_chunks, P, KT * CH)
    tok_w = a["L0_tok_W"].reshape(D, KT, P).transpose(2, 1, 0).reshape(P, KT * D)
    in_b, conv_w = a["L0_attn_in_b"], a["L0_attn_conv_w"]
    vectors = [in_b[:D], in_b[D:], conv_w[:, 0, 0], conv_w[:, 0, 1], conv_w[:, 0, 2],
               a["L0_attn_conv_b"], a["L0_attn_delta_b"], a["L0_attn_D_param"]]
    bc_w = np.concatenate([a["L0_attn_B_proj_w"], a["L0_attn_C_proj_w"]] * 3).T
    w1 = np.concatenate([a["L0_ffn_w1"], a["L0_ffn_sw1"][None]])
    w3 = np.concatenate([a["L0_ffn_w3"], a["L0_ffn_sw3"][None]])
    w2 = np.concatenate([a["L0_ffn_w2"], a["L0_ffn_sw2"][None]])
    sel = np.zeros((96, 2 * N, P), ml_dtypes.bfloat16)
    for part in range(3):
        for r in range(2 * N):
            sel[32 * part + r, r, :] = 1
    laid = {
        "x": x, "ident": np.eye(P, dtype=f32), "sel": sel,
        "cols": np.stack([twice(v) for v in vectors], axis=1).reshape(P, NCOL),
        "alphas": on_all(np.stack([a["L0_tok_alpha_a"], a["L0_tok_alpha_w"]])),
        "a_log": twice(a["L0_attn_A_log"]).reshape(P, 2 * N),
        "tok_w": tok_w, "tok_b": on_all(np.stack([a["L0_tok_b"]] * 2)),
        "out_b": on_all(np.stack([a["L0_attn_out_b"]] * TT)),
        "in_w": twice(a["L0_attn_in_w"].T), "delta_w": twice(a["L0_attn_delta_w"].T),
        "bc_w": twice(bc_w), "out_w": twice(a["L0_attn_out_w"].T),
        "gate_w": twice(a["L0_ffn_gate_weight"].T), "gate_b": on_all(np.stack([a["L0_ffn_gate_bias"]] * TT)),
        "before4": on_all(np.tril(np.ones((4, 4), f32), -1)), "before8": on_all(np.tril(np.ones((8, 8), f32), -1)),
        "w1": twice(w1.transpose(2, 0, 1)), "w3": twice(w3.transpose(2, 0, 1)), "w2": w2.transpose(2, 0, 1),
    }
    nc = bacc.Bacc("TRN2", target_bir_lowering=False, num_devices=1)
    arrays, aps = {}, {}
    for name, value in laid.items():
        value = np.ascontiguousarray(value)
        arrays[f"in_{name}_dram"] = value
        aps[name] = nc.dram_tensor(f"in_{name}_dram", value.shape, mybir.dt.from_np(value.dtype),
                                   kind="ExternalInput").ap()
    out = nc.dram_tensor("out_0_dram", (n_img, L, D), F32, kind="ExternalOutput").ap()
    out_v = out.rearrange("(c m) l d -> c (m l) d", c=n_chunks).rearrange("c (t p) d -> c p t d", p=P)
    build(nc, aps, out_v)
    got = run_bass_kernel_spmd(nc, [arrays], core_ids=[0])
    return got.results[0]["out_0_dram"]
```
